# Optimizing a Trainium2 kernel written in Bass

```python
import numpy as np
import jax
import jax.numpy as jnp

def _softmax(x, axis=-1):
    return jax.nn.softmax(x, axis=axis)

def _gelu(x):
    return jax.nn.gelu(x, approximate=True)

def _silu(x):
    return jax.nn.silu(x)

def _sigmoid(x):
    return jax.nn.sigmoid(x)

def _layernorm(x, axis=-1, eps=1e-05):
    m = jnp.mean(x, axis=axis, keepdims=True)
    v = jnp.var(x, axis=axis, keepdims=True)
    return (x - m) / jnp.sqrt(v + eps)

def _scatter_add(tgt, idx, src, axis=0):
    return tgt.at[idx].add(src)

def _segment_sum(src, seg, n):
    return jax.ops.segment_sum(src, seg, n)
kernel_name = 'mk_prb_d1_jaxref_r8_723c67'

def setup_inputs(seed: int=0):
    np.random.seed(seed)
    _w = jnp.asarray

    def _L0_attn_setup():
        import math
        import jax, jax.numpy as jnp
        import numpy as np
        LN_EPS = 1e-05

        def _relative_sinusoidal(t, hd, dtype):
            pos = jnp.arange(-(t - 1), t, dtype=dtype)[:, None]
            div = jnp.exp(jnp.arange(0, hd, 2, dtype=dtype) * (-math.log(10000.0) / hd))
            pe = jnp.zeros((2 * t - 1, hd), dtype=dtype)
            pe = pe.at[:, 0::2].set(jnp.sin(pos * div))
            pe = pe.at[:, 1::2].set(jnp.cos(pos * div))
            return pe
        key = jax.random.key(seed)
        ks = jax.random.split(key, 4)
        b, t, dim, H = (2, 256, 128, 16)
        hd = dim // H
        s = 0.02
        return {'x': jax.random.normal(ks[0], (b, t, dim), jnp.float32), 'ln_g': jnp.ones((dim,), jnp.float32), 'ln_b': jnp.zeros((dim,), jnp.float32), 'w_qkv': jax.random.normal(ks[1], (dim, 3 * dim), jnp.float32) * s, 'b_qkv': jnp.zeros((3 * dim,), jnp.float32), 'w_rel': jax.random.normal(ks[2], (hd, H), jnp.float32) * s, 'w_out': jax.random.normal(ks[3], (dim, dim), jnp.float32) * s, 'b_out': jnp.zeros((dim,), jnp.float32)}
    _L0_attn_in = _L0_attn_setup()

    def _L0_ffn_setup():
        import jax, jax.numpy as jnp
        import numpy as np
        DIM = 128

        def _reference_tuple_inner(x, W_r, W_k, W_v, mu_r, mu_k):
            B, T, C = x.shape
            x_prev = jnp.concatenate([jnp.zeros((B, 1, C), x.dtype), x[:, :-1, :]], axis=1)
            xr = mu_r * x + (1.0 - mu_r) * x_prev
            xk = mu_k * x + (1.0 - mu_k) * x_prev
            r = jax.nn.sigmoid(jnp.einsum('btc,dc->btd', xr, W_r))
            k = jnp.einsum('btc,dc->btd', xk, W_k)
            k_act = jnp.square(jax.nn.relu(k))
            out = r * jnp.einsum('btc,dc->btd', k_act, W_v)
            new_state = x[:, -1, :]
            return (out, new_state)
        key = jax.random.key(seed)
        ks = jax.random.split(key, 6)
        B, T, C = (8, 256, DIM)
        x = jax.random.normal(ks[0], (B, T, C), dtype=jnp.float32)
        s = 1.0 / np.sqrt(C)
        W_r = jax.random.uniform(ks[1], (C, C), jnp.float32, -s, s)
        W_k = jax.random.uniform(ks[2], (C, C), jnp.float32, -s, s)
        W_v = jax.random.uniform(ks[3], (C, C), jnp.float32, -s, s)
        mu_r = jax.random.uniform(ks[4], (C,), jnp.float32)
        mu_k = jax.random.uniform(ks[5], (C,), jnp.float32)
        return {'x': x, 'W_r': W_r, 'W_k': W_k, 'W_v': W_v, 'mu_r': mu_r, 'mu_k': mu_k}
    _L0_ffn_in = _L0_ffn_setup()
    _d = {'L0_attn_x': _L0_attn_in['x'], 'L0_attn_ln_g': _L0_attn_in['ln_g'], 'L0_attn_ln_b': _L0_attn_in['ln_b'], 'L0_attn_w_qkv': _L0_attn_in['w_qkv'], 'L0_attn_b_qkv': _L0_attn_in['b_qkv'], 'L0_attn_w_rel': _L0_attn_in['w_rel'], 'L0_attn_w_out': _L0_attn_in['w_out'], 'L0_attn_b_out': _L0_attn_in['b_out'], 'L0_ffn_W_r': _L0_ffn_in['W_r'], 'L0_ffn_W_k': _L0_ffn_in['W_k'], 'L0_ffn_W_v': _L0_ffn_in['W_v'], 'L0_ffn_mu_r': _L0_ffn_in['mu_r'], 'L0_ffn_mu_k': _L0_ffn_in['mu_k']}
    _x0 = _d['L0_attn_x']
    _d['L0_attn_x'] = jax.random.normal(jax.random.fold_in(jax.random.key(seed), 1), (8, 512, 128), dtype=_x0.dtype)
    del _x0
    return _d

def reference(L0_attn_x, L0_attn_ln_g, L0_attn_ln_b, L0_attn_w_qkv, L0_attn_b_qkv, L0_attn_w_rel, L0_attn_w_out, L0_attn_b_out, L0_ffn_W_r, L0_ffn_W_k, L0_ffn_W_v, L0_ffn_mu_r, L0_ffn_mu_k):

    def _L0_attn_ref(x, ln_g, ln_b, w_qkv, b_qkv, w_rel, w_out, b_out):
        import math
        import jax, jax.numpy as jnp
        import numpy as np
        LN_EPS = 1e-05

        def _relative_sinusoidal(t, hd, dtype):
            pos = jnp.arange(-(t - 1), t, dtype=dtype)[:, None]
            div = jnp.exp(jnp.arange(0, hd, 2, dtype=dtype) * (-math.log(10000.0) / hd))
            pe = jnp.zeros((2 * t - 1, hd), dtype=dtype)
            pe = pe.at[:, 0::2].set(jnp.sin(pos * div))
            pe = pe.at[:, 1::2].set(jnp.cos(pos * div))
            return pe
        b, t, dim = x.shape
        hd, H = w_rel.shape
        scale = hd ** (-0.5)
        mu = jnp.mean(x, axis=-1, keepdims=True)
        var = jnp.mean(jnp.square(x - mu), axis=-1, keepdims=True)
        xn = (x - mu) * jax.lax.rsqrt(var + LN_EPS) * ln_g + ln_b
        qkv = (xn @ w_qkv + b_qkv).reshape(b, t, 3, H, hd)
        qkv = jnp.transpose(qkv, (2, 0, 3, 1, 4))
        q, k, v = (qkv[0], qkv[1], qkv[2])
        scores = jnp.einsum('bhqd,bhkd->bhqk', q, k) * scale
        rel_pe = _relative_sinusoidal(t, hd, scores.dtype)
        rel_bias = rel_pe @ w_rel
        idx = jnp.arange(t)[:, None] - jnp.arange(t)[None, :] + (t - 1)
        bias = jnp.transpose(rel_bias[idx], (2, 0, 1))[None]
        attn = jax.nn.softmax(scores + bias, axis=-1)
        out = jnp.einsum('bhqk,bhkd->bhqd', attn, v)
        out = jnp.transpose(out, (0, 2, 1, 3)).reshape(b, t, dim)
        return out @ w_out + b_out

    def _L0_ffn_ref(x, W_r, W_k, W_v, mu_r, mu_k):
        import jax, jax.numpy as jnp
        import numpy as np
        DIM = 128

        def _reference_tuple_inner(x, W_r, W_k, W_v, mu_r, mu_k):
            B, T, C = x.shape
            x_prev = jnp.concatenate([jnp.zeros((B, 1, C), x.dtype), x[:, :-1, :]], axis=1)
            xr = mu_r * x + (1.0 - mu_r) * x_prev
            xk = mu_k * x + (1.0 - mu_k) * x_prev
            r = jax.nn.sigmoid(jnp.einsum('btc,dc->btd', xr, W_r))
            k = jnp.einsum('btc,dc->btd', xk, W_k)
            k_act = jnp.square(jax.nn.relu(k))
            out = r * jnp.einsum('btc,dc->btd', k_act, W_v)
            new_state = x[:, -1, :]
            return (out, new_state)
        return _reference_tuple_inner(x, W_r, W_k, W_v, mu_r, mu_k)[0]
    x = L0_attn_x
    xn = _layernorm(x, axis=-1)
    x = x + _L0_attn_ref(xn, L0_attn_ln_g, L0_attn_ln_b, L0_attn_w_qkv, L0_attn_b_qkv, L0_attn_w_rel, L0_attn_w_out, L0_attn_b_out) + _L0_ffn_ref(xn, L0_ffn_W_r, L0_ffn_W_k, L0_ffn_W_v, L0_ffn_mu_r, L0_ffn_mu_k)
    return x

_drawn_inputs = setup_inputs


def setup_inputs(seed=0):
    import zlib

    import numpy as np

    out = dict(_drawn_inputs(seed))
    spreads = {'L0_attn_ln_g': (1.0, 0.6),
     'L0_attn_ln_b': (0.0, 0.8),
     'L0_attn_b_qkv': (0.0, 0.337),
     'L0_attn_b_out': (0.0, 0.1)}
    factors = {'L0_attn_w_qkv': 8.0, 'L0_attn_w_rel': 8.0, 'L0_ffn_W_r': 3.164, 'L0_ffn_mu_r': 6.223}
    for name, (base, spread) in spreads.items():
        noise = np.random.default_rng([zlib.crc32(name.encode()), seed]).standard_normal(out[name].shape)
        drawn = base * np.exp(spread * noise) if base else spread * noise
        out[name] = jnp.asarray(drawn.astype(out[name].dtype))
    for name, factor in factors.items():
        out[name] = (out[name] * factor).astype(out[name].dtype)
    return out
```

```python
from contextlib import ExitStack

import numpy as np

import concourse.bass as bass
from concourse import mybir

B, T, C, H, HD = 8, 512, 128, 16, 8
P = 128
TB = T // P
G = H // 4
STEPS = G * TB
LEAD = 6
Q_PARTS = (0, 1, 2, 0, 1, 0)
K_PARTS = (0, 0, 0, 1, 1, 2)
NPROD = len(Q_PARTS)
KREL = NPROD * HD
KMAX = 2 * KREL
KROWS = KMAX + 2
VW = 32
RING = 16
EPS = 1e-5
SCALE = HD ** -0.5
W_Q, W_K, W_V, W_R, W_KF, W_VF, W_O = range(7)
C_G, C_B, C_BQ, C_BK, C_MUR, C_MUK, C_WS, C_WC = range(8)

PLAN = {
    1: [("o3", "prev"), ("xnT", "next")],
    2: [("m1", "this"), ("xaT", "next")],
    3: [("onT", "prev"), ("q", "next")],
    4: [("out", "prev"), ("k", "next")],
    5: [("o0", "this"), ("v", "next")],
    6: [("m2", "this"), ("r", "next")],
    7: [None, ("kf", "next")],
    8: [None, ("kv", "next")],
    9: [("o1", "this"), None],
    10: [("m3", "this"), None],
    13: [("o2", "this"), None],
    14: [("m0", "next"), None],
}


def plan(kind, unit):
    drop = {"first": "prev", "middle": None, "last": "next"}[kind]
    return [u if u is not None and u[1] != drop else None for u in PLAN.get(unit, [None, None])]


def build(nc, x, weights, cols, rows, rel_tab, k_rel, ident_f, ident_b, out, scratch):
    fp32, bf16, i32 = mybir.dt.float32, mybir.dt.bfloat16, mybir.dt.int32
    ALU, ACT, AX = mybir.AluOpType, mybir.ActivationFunctionType, mybir.AxisListType

    ctx = ExitStack()
    with ctx:
        def sb(name, shape, dt=fp32):
            return ctx.enter_context(nc.sbuf_tensor(name, shape, dt))

        def sem(name):
            return ctx.enter_context(nc.semaphore(name))

        w_sb = sb("w_sb", [P, 7, C])
        c_sb = sb("c_sb", [P, 8])
        bq_scaled = sb("bq_scaled", [P, 1])
        mu_rest = sb("mu_rest", [P, 2])
        row_sb = sb("row_sb", [P, 2, C])
        idf = sb("idf", [P, P])
        idb = sb("idb", [P, P], bf16)
        tab = sb("tab", [P, 2, T])
        x_all = sb("x_all", [P, B, TB, C])
        stats = sb("stats", [P, B, TB, 6])
        moments = sb("moments", [P, B * TB, 2])
        lnw = sb("lnw", [P, 2, B * TB])
        lny = sb("lny", [P, 2, B * TB])
        lnt = sb("lnt", [P, 2, B * TB])
        xn_tok = sb("xn_tok", [P, TB, C])
        xa_tok = sb("xa_tok", [P, TB, C])
        xnT = sb("xnT", [P, 1 + T])
        xaT = sb("xaT", [P, T])
        full = [sb(f"full_{n}", [P, T]) for n in "qk"]
        left = [sb(f"left_{n}", [P, T]) for n in "qk"]
        parts = [sb(f"parts_{n}", [P, 3, T], bf16) for n in "qk"]
        Q = sb("Q", [KROWS, H, T], bf16)
        K = sb("K", [KROWS, H, T], bf16)
        negmax = sb("negmax", [P, 2, 16])
        nm_left = sb("nm_left", [P, 16])
        nm_parts = sb("nm_parts", [P, 2, 16], bf16)
        nm_rows = sb("nm_rows", [32, 2, P], bf16)
        v_stage = sb("v_stage", [P, TB, C])
        V = sb("V", [P, TB, H, VW])
        probs = sb("probs", [P, RING, T])
        o_raw = sb("o_raw", [P, T])
        rsum = sb("rsum", [P, 2, TB, 4])
        o_n = sb("o_n", [P, TB, C])
        oT = sb("oT", [P, T])
        mix_a = sb("mix_a", [P, T])
        mix_b = sb("mix_b", [P, T])
        xrT = sb("xrT", [P, T])
        xkT = sb("xkT", [P, T])
        th = sb("th", [P, TB, C])
        gate = sb("gate", [P, TB, C])
        relu = sb("relu", [P, T])
        kact = sb("kact", [P, T])
        ffn = sb("ffn", [P, TB, C])
        xb = sb("xb", [P, TB, C])
        res_next = sb("res_next", [P, TB, C])
        res = sb("res", [P, TB, C])
        y_sb = sb("y_sb", [P, TB, C])

        max_ps = ctx.enter_context(nc.psum_tensor("max_ps", [P, 2, T], fp32))
        sc_ps = ctx.enter_context(nc.psum_tensor("sc_ps", [P, 4, T], fp32))
        av_ps = ctx.enter_context(nc.psum_tensor("av_ps", [P, T], fp32))
        sh_ps = ctx.enter_context(nc.psum_tensor("sh_ps", [P, T], fp32))
        sh_tok = sh_ps[:, :].rearrange("p (j c) -> p j c", j=TB)
        sh_heads = sh_ps[:, :].rearrange("p (j h w) -> p j h w", j=TB, w=VW)
        sh_m = sh_ps[0:32, 0:P // 2].bitcast(bf16)

        x_first_loaded = sem("x_first_loaded")
        x_rest_loaded = sem("x_rest_loaded")
        cols_loaded = sem("cols_loaded")
        weights_loaded = sem("weights_loaded")
        tables_loaded = sem("tables_loaded")
        ident_loaded = sem("ident_loaded")
        krel_loaded = sem("krel_loaded")
        qrel_written = sem("qrel_written")
        qrel_loaded = sem("qrel_loaded")
        scratch_written = sem("scratch_written")
        slab_loaded = [sem(f"slab{g}_loaded") for g in range(G)]
        m_loaded = [sem(f"m{g}_loaded") for g in range(G)]
        y_stored = sem("y_stored")
        max_tile = sem("max_tile")
        score_tile = sem("score_tile")
        av_step = sem("av_step")
        xnT_made = sem("xnT_made")
        xaT_made = sem("xaT_made")
        q_made = sem("q_made")
        k_made = sem("k_made")
        v_made = sem("v_made")
        r_made = sem("r_made")
        kf_made = sem("kf_made")
        kv_made = sem("kv_made")
        m_made = sem("m_made")
        o_made = sem("o_made")
        onT_made = sem("onT_made")
        out_made = sem("out_made")
        rows_maxed = sem("rows_maxed")
        probs_ready = sem("probs_ready")
        small_ready = sem("small_ready")
        zeros_ready = sem("zeros_ready")
        ln_chain = sem("ln_chain")
        xn_ready = sem("xn_ready")
        xa_ready = sem("xa_ready")
        xnT_ready = sem("xnT_ready")
        xaT_ready = sem("xaT_ready")
        full_ready = [sem(f"full_{n}_ready") for n in "qk"]
        split_chain = [sem(f"split_{n}_chain") for n in "qk"]
        parts_ready = [sem(f"parts_{n}_ready") for n in "qk"]
        rel_full_ready = sem("rel_full_ready")
        rel_chain = sem("rel_chain")
        rel_parts_ready = sem("rel_parts_ready")
        m_chain = sem("m_chain")
        m_split = sem("m_split")
        m_rows = sem("m_rows")
        v_staged = sem("v_staged")
        v_ready = sem("v_ready")
        mix_chain = sem("mix_chain")
        xr_ready = sem("xr_ready")
        xk_ready = sem("xk_ready")
        th_ready = sem("th_ready")
        relu_ready = sem("relu_ready")
        gate_ready = sem("gate_ready")
        kact_ready = sem("kact_ready")
        xb_ready = sem("xb_ready")
        ffn_ready = sem("ffn_ready")
        res_next_ready = sem("res_next_ready")
        res_ready = sem("res_ready")
        o_raw_ready = sem("o_raw_ready")
        rsum_ready = sem("rsum_ready")
        o_n_ready = sem("o_n_ready")
        oT_ready = sem("oT_ready")
        y_ready = sem("y_ready")
        waited = sem("waited")

        block = ctx.enter_context(nc.Block())

        def bodies(eng, body):
            body("first", 0)
            with eng.Fori(1, B - 1) as b:
                body("middle", b)
            body("last", B - 1)

        def chain(eng, sem_, base):
            done = [base]

            def link(ins):
                ins.then_inc(sem_, 1)
                done[0] = done[0] + 1
                eng.wait_ge(sem_, done[0])
            return link

        def positive(v):
            return not isinstance(v, int) or v > 0

        def settle(eng):
            eng.sem_inc(waited, 1)

        @block.sync
        def _(sp):
            def write_scratch(n):
                sp.dma_start(scratch[n].rearrange("a p t -> p a t"), parts[n][:, :, :]).then_inc(scratch_written, 16)

            def load_slab(g):
                hs = slice(4 * g, 4 * g + 4)
                src = scratch.rearrange("n a (d h) t -> n a d h t", h=H)[:, :, :, hs, :]
                for rows_, part in ((0, slice(0, 3)), (3, slice(0, 2)), (5, slice(0, 1))):
                    n = part.stop - part.start
                    sp.dma_start(Q[rows_ * HD:(rows_ + n) * HD, hs, :],
                                 src[0, part].rearrange("a d h t -> (a d) h t")).then_inc(slab_loaded[g], 16)
                for row, part in enumerate(K_PARTS):
                    sp.dma_start(K[row * HD:(row + 1) * HD, hs, :], src[1, part]).then_inc(slab_loaded[g], 16)

            def load_m(g, b):
                sp.wait_ge(m_rows, 4 * b + g + 1)
                settle(sp)
                after = (b - 1) * 4 * STEPS + 16 * (g + 1)
                if positive(after):
                    sp.wait_ge(score_tile, after)
                    settle(sp)
                for p in range(2):
                    sp.dma_start(Q[KMAX + p:KMAX + p + 1, 4 * g:4 * g + 4, :],
                                 nm_rows[16 * p:16 * p + 16, g % 2, :]).then_inc(m_loaded[g], 16)

            def slab(g, b):
                after = (b - 1) * 4 * STEPS + 16 * (g + 1)
                if positive(after):
                    sp.wait_ge(score_tile, after)
                    settle(sp)
                load_slab(g)

            def store(b):
                sp.wait_ge(y_ready, b + 1)
                settle(sp)
                sp.dma_start(out[bass.ds(b, 1)].rearrange("o (j p) c -> p (o j) c", p=P), y_sb[:, :, :]).then_inc(y_stored, 16)

            sp.dma_start(x_all[:, 0], x[0].rearrange("(j p) c -> p j c", p=P)).then_inc(x_first_loaded, 16)
            sp.dma_start(idf[:, :], ident_f).then_inc(ident_loaded, 16)
            sp.dma_start(idb[:, :], ident_b).then_inc(ident_loaded, 16)
            sp.dma_start(c_sb[:, :], cols).then_inc(cols_loaded, 16)
            sp.dma_start(w_sb[:, :, :], weights).then_inc(weights_loaded, 16)
            sp.dma_start(tab[:, :, :], rel_tab).then_inc(tables_loaded, 16)
            sp.dma_start(row_sb[:, :, :], rows.partition_broadcast(P)).then_inc(tables_loaded, 16)
            sp.dma_start(K[KREL:KROWS, :, :], k_rel[:, None, :].to_broadcast([KROWS - KREL, H, T])).then_inc(krel_loaded, 16)
            sp.dma_start(x_all[:, 1:], x[1:].rearrange("b (j p) c -> p b j c", p=P)).then_inc(x_rest_loaded, 16)
            sp.wait_ge(rel_parts_ready, 1)
            write_scratch(0)
            sp.wait_ge(scratch_written, 16)
            rel = scratch[0].rearrange("a (d h) t -> a d h t", h=H)
            for rows_, n in ((0, 3), (3, 2), (5, 1)):
                sp.dma_start(Q[KREL + rows_ * HD:KREL + (rows_ + n) * HD, :, :],
                             rel[0:n].rearrange("a d h t -> (a d) h t")).then_inc(qrel_loaded, 16)
            sp.wait_ge(qrel_loaded, 48)
            sp.wait_ge(parts_ready[0], 1)
            write_scratch(0)
            sp.wait_ge(parts_ready[1], 1)
            write_scratch(1)
            sp.wait_ge(scratch_written, 48)
            for g in range(G):
                load_slab(g)
            load_m(0, 0)

            def body(kind, b):
                load_m(1, b)
                if kind != "first":
                    store(b - 1)
                load_m(2, b)
                if kind == "last":
                    load_m(3, b)
                    return
                for g in range(G):
                    sp.wait_ge(slab_loaded[g], 9 * 16 * (b + 1))
                    settle(sp)
                for n in range(2):
                    sp.wait_ge(parts_ready[n], b + 2)
                    settle(sp)
                    write_scratch(n)
                sp.wait_ge(scratch_written, 32 * (b + 2) + 16)
                settle(sp)
                slab(0, b + 1)
                slab(1, b + 1)
                load_m(3, b)
                slab(2, b + 1)
                load_m(0, b + 1)
                slab(3, b + 1)

            bodies(sp, body)
            store(B - 1)
            sp.wait_ge(y_stored, 16 * B)

        @block.tensor
        def _(pe):
            last_use = []

            def take_bank(name, b):
                if last_use:
                    before, of = last_use
                    count = of + 1
                    if before[0] == "m":
                        done, count = m_rows, 4 * of + int(before[1]) + 1
                    elif before[0] == "o" and before[1].isdigit():
                        done, count = o_n_ready, 4 * of + int(before[1]) + 1
                    else:
                        done = {"xnT": xnT_ready, "xaT": xaT_ready, "q": full_ready[0], "k": full_ready[1],
                                "v": v_staged, "r": th_ready, "kf": relu_ready, "kv": ffn_ready,
                                "onT": oT_ready, "out": y_ready}[before]
                    pe.wait_ge(done, count)
                last_use[:] = name, b

            def transposes(src, made):
                for j in range(TB):
                    last = nc.tensor.transpose(sh_ps[:, j * P:(j + 1) * P], src[:, j * P:(j + 1) * P], idf[:, :])
                last.then_inc(made, 1)

            def by_token(lhs, w, made):
                for j in range(TB):
                    last = nc.tensor.matmul(sh_ps[:, j * P:(j + 1) * P], lhs[:, j * P:(j + 1) * P],
                                            w_sb[:, w, :], start=True, stop=True)
                last.then_inc(made, 1)

            def by_channel(w, rhs, made):
                nc.tensor.matmul(sh_ps[:, :], w_sb[:, w, :], rhs[:, :], start=True, stop=True).then_inc(made, 1)

            flat = "p j c -> p (j c)"

            def use(name, b):
                take_bank(name, b)
                if name == "xnT":
                    pe.wait_ge(xn_ready, 4 * (b + 1))
                    transposes(xn_tok[:, :, :].rearrange(flat), xnT_made)
                elif name == "xaT":
                    pe.wait_ge(xa_ready, 4 * (b + 1))
                    transposes(xa_tok[:, :, :].rearrange(flat), xaT_made)
                elif name == "q":
                    pe.wait_ge(xaT_ready, b + 1)
                    by_channel(W_Q, xaT, q_made)
                elif name == "k":
                    by_channel(W_K, xaT, k_made)
                elif name == "v":
                    by_token(xaT, W_V, v_made)
                elif name == "r":
                    pe.wait_ge(xr_ready, b + 1)
                    by_token(xrT, W_R, r_made)
                elif name == "kf":
                    pe.wait_ge(xk_ready, b + 1)
                    by_channel(W_KF, xkT, kf_made)
                elif name == "kv":
                    pe.wait_ge(kact_ready, b + 1)
                    by_token(kact, W_VF, kv_made)
                elif name[0] == "m":
                    pe.wait_ge(m_split, 4 * b + int(name[1]) + 1)
                    nc.tensor.transpose(sh_m, nm_parts[:, :, :].rearrange("p a n -> p (a n)"),
                                        idb[:, :]).then_inc(m_made, 1)
                elif name == "onT":
                    pe.wait_ge(o_n_ready, 4 * (b + 1))
                    transposes(o_n[:, :, :].rearrange(flat), onT_made)
                elif name == "out":
                    pe.wait_ge(oT_ready, b + 1)
                    by_token(oT, W_O, out_made)
                else:
                    pe.wait_ge(o_raw_ready, 4 * b + int(name[1]) + 1)
                    transposes(o_raw, o_made)

            def max_tile_of(pos, b, i):
                g, head = pos // 4, pos
                n = b * 4 * STEPS + 4 * pos + i
                if pos % 4 == 0 and i == 0:
                    pe.wait_ge(slab_loaded[g], 9 * 16 * (b + 1))
                if positive(n - 1):
                    pe.wait_ge(rows_maxed, n - 1)
                nc.tensor.matmul(max_ps[:, i % 2, :], Q[0:KMAX, head, i * P:(i + 1) * P], K[0:KMAX, head, :],
                                 start=True, stop=True).then_inc(max_tile, 1)

            def score_tile_of(s, b, i):
                g, kt = s // 4, s % 4
                n = b * 4 * STEPS + 4 * s + i
                if kt == 0 and i == 0:
                    pe.wait_ge(m_loaded[g], 32 * (b + 1))
                if positive(n - 3):
                    pe.wait_ge(probs_ready, n - 3)
                head = 4 * g + i
                nc.tensor.matmul(sc_ps[:, i, :], K[:, head, kt * P:(kt + 1) * P], Q[:, head, :],
                                 start=True, stop=True).then_inc(score_tile, 1)

            def av(s, b):
                g, kt = s // 4, s % 4
                pe.wait_ge(probs_ready, b * 4 * STEPS + 4 * s + 4)
                if kt == 0:
                    pe.wait_ge(v_ready, 4 * b + g + 1)
                    if positive(4 * b + g):
                        pe.wait_ge(o_raw_ready, 4 * b + g)
                for i in range(4):
                    last = nc.tensor.matmul(av_ps[VW * i:VW * (i + 1), :], V[:, kt, 4 * g + i, :],
                                            probs[:, (4 * s + i) % RING, :], start=kt == 0, stop=kt == TB - 1)
                last.then_inc(av_step, 1)

            pe.wait_ge(ident_loaded, 32)
            for name in ("xnT", "xaT"):
                use(name, 0)
            pe.wait_ge(weights_loaded, 16)
            for name in ("q", "k", "v", "r", "kf", "kv"):
                use(name, 0)
            pe.wait_ge(krel_loaded, 16)
            pe.wait_ge(qrel_loaded, 48)
            for pos in range(LEAD):
                for i in range(4):
                    max_tile_of(pos, 0, i)
                if pos == 4:
                    use("m0", 0)

            def body(kind, b):
                of = {"prev": b - 1, "this": b, "next": b + 1}
                last_use[:] = "m0", b
                for s in range(STEPS):
                    shared = plan(kind, s)
                    for i in range(4):
                        ahead = s + LEAD
                        if ahead < STEPS:
                            max_tile_of(ahead, b, i)
                        elif kind != "last":
                            max_tile_of(ahead - STEPS, b + 1, i)
                        score_tile_of(s, b, i)
                        if i in (0, 2) and shared[i // 2] is not None:
                            name, whose = shared[i // 2]
                            use(name, of[whose])
                        if i == 1 and s > 0:
                            av(s - 1, b)
                        elif i == 1 and kind != "first":
                            av(STEPS - 1, b - 1)

            bodies(pe, body)
            av(STEPS - 1, B - 1)
            for name in ("o3", "onT", "out"):
                use(name, B - 1)

        @block.scalar
        def _(act):
            def exp_tile(s, b, i):
                n = b * 4 * STEPS + 4 * s + i
                if i == 0:
                    before = b * STEPS + s - RING // 4 + 1
                    if positive(before):
                        act.wait_ge(av_step, before)
                act.wait_ge(score_tile, n + 1)
                nc.scalar.activation(probs[:, (4 * s + i) % RING, :], sc_ps[:, i, :], ACT.Exp).then_inc(probs_ready, 1)

            def read_av(s, b):
                act.wait_ge(av_step, b * STEPS + s + 1)
                n = 4 * b + s // 4
                if positive(n):
                    act.wait_ge(o_made, n)
                nc.scalar.copy(o_raw[:, :], av_ps[:, :]).then_inc(o_raw_ready, 1)

            def read_out(name, b):
                if name == "xnT":
                    act.wait_ge(xnT_made, b + 1)
                    if positive(b):
                        act.wait_ge(xk_ready, b)
                    ins, done = nc.scalar.copy(xnT[:, 1:], sh_ps[:, :]), xnT_ready
                elif name == "xaT":
                    act.wait_ge(xaT_made, b + 1)
                    if positive(b):
                        act.wait_ge(v_made, b)
                    ins, done = nc.scalar.activation(xaT[:, :], sh_ps[:, :], ACT.Identity, bias=c_sb[:, C_B:C_B + 1],
                                                     scale=c_sb[:, C_G:C_G + 1]), xaT_ready
                elif name in ("q", "k"):
                    n = "qk".index(name)
                    act.wait_ge((q_made, k_made)[n], b + 1)
                    if positive(b):
                        act.wait_ge(parts_ready[n], b)
                    bias = (bq_scaled[:, 0:1], c_sb[:, C_BK:C_BK + 1])[n]
                    ins, done = nc.scalar.activation(full[n][:, :], sh_ps[:, :], ACT.Identity, bias=bias,
                                                     scale=(SCALE, 1.0)[n]), full_ready[n]
                elif name == "r":
                    act.wait_ge(r_made, b + 1)
                    if positive(b):
                        act.wait_ge(gate_ready, b)
                    ins, done = nc.scalar.activation(th[:, :, :], sh_tok, ACT.Tanh, scale=0.5), th_ready
                elif name == "kf":
                    act.wait_ge(kf_made, b + 1)
                    if positive(b):
                        act.wait_ge(kact_ready, b)
                    ins, done = nc.scalar.activation(relu[:, :], sh_ps[:, :], ACT.Relu), relu_ready
                elif name == "onT":
                    act.wait_ge(onT_made, b + 1)
                    if positive(b):
                        act.wait_ge(out_made, b)
                    ins, done = nc.scalar.copy(oT[:, :], sh_ps[:, :]), oT_ready
                elif name[0] == "m":
                    g = int(name[1])
                    act.wait_ge(m_made, 4 * b + g + 1)
                    before = b if g >= 2 else b - 1
                    if positive(before + (g >= 2)):
                        act.wait_ge(m_loaded[(g + 2) % 4], 32 * (before + 1))
                    ins, done = nc.scalar.copy(nm_rows[:, g % 2, :], sh_m), m_rows
                else:
                    return
                ins.then_inc(done, 1)

            act.wait_ge(cols_loaded, 16)
            act.wait_ge(small_ready, 3)
            for name in ("xnT", "xaT", "q", "k", "r", "kf", "m0"):
                read_out(name, 0)

            def body(kind, b):
                of = {"prev": b - 1, "this": b, "next": b + 1}
                for s in range(STEPS):
                    shared = plan(kind, s)
                    exp_tile(s, b, 0)
                    if shared[0] is not None:
                        read_out(shared[0][0], of[shared[0][1]])
                    exp_tile(s, b, 1)
                    exp_tile(s, b, 2)
                    if s % 4 == 0 and s > 0:
                        read_av(s - 1, b)
                    elif s == 0 and kind != "first":
                        read_av(STEPS - 1, b - 1)
                    if shared[1] is not None:
                        read_out(shared[1][0], of[shared[1][1]])
                    exp_tile(s, b, 3)

            bodies(act, body)
            read_av(STEPS - 1, B - 1)
            read_out("onT", B - 1)

        @block.vector
        def _(dve):
            ln = chain(dve, ln_chain, 0)

            def statistics(bs):
                for b in bs:
                    for j in range(TB):
                        last = nc.vector.bn_stats(stats[:, b, j, :], x_all[:, b, j, :])
                ln(last)
                n0, n1 = bs[0] * TB, (bs[-1] + 1) * TB
                for b in bs:
                    for j in range(TB):
                        last = nc.vector.bn_aggr(moments[:, b * TB + j, :], stats[:, b, j, :])
                ln(last)
                var = moments[:, n0:n1, 1]
                w, y, t = (a[:, :, n0:n1] for a in (lnw, lny, lnt))
                nc.vector.tensor_scalar(lnw[:, 0, n0:n1], var, EPS, None, ALU.add)
                ln(nc.vector.tensor_scalar(lnw[:, 1, n0:n1], var, 1.0 + EPS, EPS * EPS, ALU.mult, ALU.add))
                ln(nc.vector.tensor_scalar(y.bitcast(i32), w.bitcast(i32), -0.5, float(0x5f3759df), ALU.mult, ALU.add))
                for _ in range(4):
                    ln(nc.vector.scalar_tensor_tensor(t, y, -0.5, y, ALU.mult, ALU.mult))
                    ln(nc.vector.tensor_tensor(t, t, w, ALU.mult))
                    ln(nc.vector.scalar_tensor_tensor(y, t, 1.5, y, ALU.add, ALU.mult))

            def normalise(b, which):
                if positive(b):
                    dve.wait_ge((xnT_made, xaT_made)[which], b)
                dst = (xn_tok, xa_tok)[which]
                for j in range(TB):
                    n = b * TB + j
                    nc.vector.tensor_scalar(dst[:, j, :], x_all[:, bass.ds(b, 1), j, :].rearrange("p o c -> p (o c)"),
                                            moments[:, bass.ds(n, 1), 0], lny[:, which, bass.ds(n, 1)],
                                            ALU.subtract, ALU.mult).then_inc((xn_ready, xa_ready)[which], 1)

            def reduce_tile(pos, b, i):
                n = b * 4 * STEPS + 4 * pos + i
                g = pos // 4
                if pos % 4 == 0 and i == 0:
                    before = 4 * b + g - 1
                    if positive(before):
                        dve.wait_ge(m_split, before)
                dve.wait_ge(max_tile, n + 1)
                col = 4 * (pos % 4) + i
                nc.vector.tensor_reduce(negmax[:, g % 2, col:col + 1], max_ps[:, i % 2, :], AX.X, ALU.max,
                                        negate=True).then_inc(rows_maxed, 1)

            def read_out(name, b):
                if name == "v":
                    dve.wait_ge(v_made, b + 1)
                    if positive(4 * b):
                        dve.wait_ge(v_ready, 4 * b)
                    ins = nc.vector.tensor_tensor(v_stage[:, :, :], sh_tok,
                                                  row_sb[:, 0:1, :].to_broadcast([P, TB, C]), ALU.add)
                    ins.then_inc(v_staged, 1)
                elif name == "kv":
                    dve.wait_ge(kv_made, b + 1)
                    dve.wait_ge(gate_ready, b + 1)
                    if positive(b):
                        dve.wait_ge(res_next_ready, b)
                    ins = nc.vector.tensor_tensor(ffn[:, :, :], sh_tok, gate[:, :, :], ALU.mult)
                    ins.then_inc(ffn_ready, 1)
                elif name == "out":
                    dve.wait_ge(out_made, b + 1)
                    dve.wait_ge(res_ready, b + 1)
                    if positive(b):
                        dve.wait_ge(y_stored, 16 * b)
                    ins = nc.vector.tensor_tensor(y_sb[:, :, :], sh_tok, res[:, :, :], ALU.add)
                    ins.then_inc(y_ready, 1)
                elif name[0] == "o" and name != "onT":
                    g = int(name[1])
                    dve.wait_ge(o_made, 4 * b + g + 1)
                    nc.vector.reciprocal(rsum[:, g % 2], sh_heads[:, :, :, HD]).then_inc(rsum_ready, 1)
                    if g == 0 and positive(b):
                        dve.wait_ge(onT_made, b)
                    dve.wait_ge(rsum_ready, 4 * b + g + 1)
                    heads = o_n[:, :, :].rearrange("p j (h d) -> p j h d", d=HD)[:, :, 4 * g:4 * g + 4, :]
                    ins = nc.vector.tensor_tensor(heads, sh_heads[:, :, :, 0:HD],
                                                  rsum[:, g % 2][:, :, :, None].to_broadcast([P, TB, 4, HD]), ALU.mult)
                    ins.then_inc(o_n_ready, 1)

            dve.wait_ge(x_first_loaded, 16)
            statistics([0])
            normalise(0, 1)
            normalise(0, 0)
            dve.wait_ge(cols_loaded, 16)
            nc.vector.tensor_scalar(bq_scaled[:, :], c_sb[:, C_BQ:C_BQ + 1], SCALE, None, ALU.mult).then_inc(small_ready, 1)
            for n, c in enumerate((C_MUR, C_MUK)):
                nc.vector.tensor_scalar(mu_rest[:, n:n + 1], c_sb[:, c:c + 1], -1.0, 1.0, ALU.mult,
                                        ALU.add).then_inc(small_ready, 1)
            dve.wait_ge(tables_loaded, 32)
            rel = chain(dve, rel_full_ready, 0)
            rel(nc.vector.tensor_scalar(left[0][:, :], tab[:, 1, :], c_sb[:, C_WC:C_WC + 1], None, ALU.mult))
            rel(nc.vector.scalar_tensor_tensor(kact[:, :], tab[:, 0, :], c_sb[:, C_WS:C_WS + 1], left[0][:, :],
                                               ALU.mult, ALU.add))
            rel(nc.vector.tensor_copy(parts[0][:, 0, :], kact[:, :]))
            rel(nc.vector.tensor_tensor(left[0][:, :], kact[:, :], parts[0][:, 0, :], ALU.subtract))
            rel(nc.vector.tensor_copy(parts[0][:, 1, :], left[0][:, :]))
            nc.vector.tensor_tensor(parts[0][:, 2, :], left[0][:, :], parts[0][:, 1, :],
                                    ALU.subtract).then_inc(rel_parts_ready, 1)
            read_out("v", 0)
            dve.wait_ge(x_rest_loaded, 16)
            statistics(list(range(1, B)))
            read_out("kv", 0)
            for pos in range(LEAD):
                for i in range(4):
                    reduce_tile(pos, 0, i)

            def body(kind, b):
                of = {"prev": b - 1, "this": b, "next": b + 1}
                for s in range(STEPS):
                    shared = plan(kind, s)
                    for i in range(4):
                        ahead = s + LEAD
                        if ahead < STEPS:
                            reduce_tile(ahead, b, i)
                        elif kind != "last":
                            reduce_tile(ahead - STEPS, b + 1, i)
                        if i in (0, 2) and shared[i // 2] is not None:
                            read_out(shared[i // 2][0], of[shared[i // 2][1]])
                    if kind != "last" and s in (0, 1):
                        normalise(b + 1, s)

            bodies(dve, body)
            read_out("o3", B - 1)
            read_out("out", B - 1)

        @block.gpsimd
        def _(pool):
            def cast(dst, src):
                settle(pool)
                return nc.gpsimd.tensor_scalar(dst, src, 1.0, 0.0, ALU.mult, ALU.add)

            def split(n, b):
                pool.wait_ge(full_ready[n], b + 1)
                pool.wait_ge(scratch_written, 16 + 32 * b)
                settle(pool)
                link = chain(pool, split_chain[n], 3 * b)
                f, r, p = full[n], left[n], parts[n]
                link(cast(p[:, 0, :], f[:, :]))
                link(nc.gpsimd.tensor_tensor(r[:, :], f[:, :], p[:, 0, :], ALU.subtract))
                link(cast(p[:, 1, :], r[:, :]))
                nc.gpsimd.tensor_tensor(p[:, 2, :], r[:, :], p[:, 1, :], ALU.subtract).then_inc(parts_ready[n], 1)

            def split_maxima(g, b):
                n = 4 * b + g
                pool.wait_ge(rows_maxed, b * 4 * STEPS + 16 * (g + 1))
                if positive(n):
                    pool.wait_ge(m_made, n)
                settle(pool)
                link = chain(pool, m_chain, 2 * n)
                src = negmax[:, g % 2, :]
                link(cast(nm_parts[:, 0, :], src))
                link(nc.gpsimd.tensor_tensor(nm_left[:, :], src, nm_parts[:, 0, :], ALU.subtract))
                cast(nm_parts[:, 1, :], nm_left[:, :]).then_inc(m_split, 1)

            def place_v(g, b):
                pool.wait_ge(v_staged, b + 1)
                after = (b - 1) * STEPS + 4 * (g + 1)
                if positive(after):
                    pool.wait_ge(av_step, after)
                settle(pool)
                for j in range(TB):
                    last = cast(V[:, j, 4 * g:4 * g + 4, 0:HD],
                                v_stage[:, j, 4 * HD * g:4 * HD * (g + 1)].rearrange("p (h d) -> p h d", d=HD))
                last.then_inc(v_ready, 1)

            def mix(b):
                pool.wait_ge(xnT_ready, b + 1)
                link = chain(pool, mix_chain, 2 * b)
                for n, (mu, dst, made, ready) in enumerate(((C_MUR, xrT, r_made, xr_ready), (C_MUK, xkT, kf_made, xk_ready))):
                    if n == 1:
                        pool.wait_ge(xr_ready, b + 1)
                    elif positive(b):
                        pool.wait_ge(xk_ready, b)
                    settle(pool)
                    nc.gpsimd.tensor_scalar(mix_a[:, :], xnT[:, 1:], c_sb[:, mu:mu + 1], 0.0, ALU.mult, ALU.add)
                    link(nc.gpsimd.tensor_scalar(mix_b[:, :], xnT[:, 0:T], mu_rest[:, n:n + 1], 0.0, ALU.mult, ALU.add))
                    if positive(b):
                        pool.wait_ge(made, b)
                    nc.gpsimd.tensor_tensor(dst[:, :], mix_a[:, :], mix_b[:, :], ALU.add).then_inc(ready, 1)

            def x_and_bias(b):
                if positive(b):
                    pool.wait_ge(res_next_ready, b)
                nc.gpsimd.tensor_tensor(xb[:, :, :], x_all[:, bass.ds(b, 1)].rearrange("p o j c -> p (o j) c"),
                                        row_sb[:, 1:2, :].to_broadcast([P, TB, C]), ALU.add).then_inc(xb_ready, 1)

            def gate_of(b):
                pool.wait_ge(th_ready, b + 1)
                if positive(b):
                    pool.wait_ge(ffn_ready, b)
                settle(pool)
                nc.gpsimd.tensor_scalar(gate[:, :, :], th[:, :, :], 0.5, 0.5, ALU.mult, ALU.add).then_inc(gate_ready, 1)

            def square(b):
                pool.wait_ge(relu_ready, b + 1)
                if positive(b):
                    pool.wait_ge(kv_made, b)
                nc.gpsimd.tensor_tensor(kact[:, :], relu[:, :], relu[:, :], ALU.mult).then_inc(kact_ready, 1)

            def residual(b):
                pool.wait_ge(ffn_ready, b + 1)
                pool.wait_ge(xb_ready, b + 1)
                if positive(b):
                    pool.wait_ge(res_ready, b)
                nc.gpsimd.tensor_tensor(res_next[:, :, :], ffn[:, :, :], xb[:, :, :], ALU.add).then_inc(res_next_ready, 1)

            def hand_over(b):
                pool.wait_ge(res_next_ready, b + 1)
                if positive(b):
                    pool.wait_ge(y_ready, b)
                settle(pool)
                cast(res[:, :, :], res_next[:, :, :]).then_inc(res_ready, 1)

            nc.gpsimd.memset(xnT[:, 0:1], 0.0).then_inc(zeros_ready, 1)
            nc.gpsimd.memset(V[:, :, :, HD:VW], 0.0).then_inc(zeros_ready, 1)
            pool.wait_ge(zeros_ready, 2)
            nc.gpsimd.memset(V[:, :, :, HD:HD + 1], 1.0).then_inc(zeros_ready, 1)
            pool.wait_ge(zeros_ready, 3)
            pool.wait_ge(rel_parts_ready, 1)
            split(0, 0)
            split(1, 0)
            pool.wait_ge(small_ready, 3)
            mix(0)
            for g in range(G):
                place_v(g, 0)
            gate_of(0)
            square(0)
            x_and_bias(0)
            residual(0)
            split_maxima(0, 0)

            def body(kind, b):
                if kind != "first":
                    place_v(3, b)
                split_maxima(1, b)
                if kind != "last":
                    mix(b + 1)
                    split(0, b + 1)
                split_maxima(2, b)
                if kind != "last":
                    split(1, b + 1)
                hand_over(b)
                if kind != "last":
                    place_v(0, b + 1)
                    gate_of(b + 1)
                    square(b + 1)
                    x_and_bias(b + 1)
                    residual(b + 1)
                    place_v(1, b + 1)
                split_maxima(3, b)
                if kind != "last":
                    place_v(2, b + 1)
                    split_maxima(0, b + 1)

            bodies(pool, body)


def kernel(L0_attn_x, L0_attn_ln_g, L0_attn_ln_b, L0_attn_w_qkv, L0_attn_b_qkv, L0_attn_w_rel, L0_attn_w_out,
           L0_attn_b_out, L0_ffn_W_r, L0_ffn_W_k, L0_ffn_W_v, L0_ffn_mu_r, L0_ffn_mu_k):
    import ml_dtypes

    import concourse.bacc as bacc
    from concourse.bass_utils import run_bass_kernel_spmd

    bf = ml_dtypes.bfloat16
    a = np.asarray
    w = a(L0_attn_w_qkv).reshape(C, 3, H, HD)
    bias = a(L0_attn_b_qkv).reshape(3, H, HD)
    dim_major = lambda m: np.swapaxes(m, -1, -2).reshape(*m.shape[:-2], C)
    weights = np.stack([dim_major(w[:, 0]), dim_major(w[:, 1]), w[:, 2].reshape(C, C), a(L0_ffn_W_r).T,
                        a(L0_ffn_W_k).T, a(L0_ffn_W_v).T, a(L0_attn_w_out)], axis=1)
    rel = np.repeat(a(L0_attn_w_rel).reshape(HD // 2, 2, H), 2, axis=0)
    cols = np.stack([a(L0_attn_ln_g), a(L0_attn_ln_b), dim_major(bias[0]), dim_major(bias[1]), a(L0_ffn_mu_r),
                     a(L0_ffn_mu_k), rel[:, 0].reshape(C), rel[:, 1].reshape(C)], axis=1)
    rows = np.stack([bias[2].reshape(C), a(L0_attn_b_out)])

    div = np.exp(np.arange(0, HD, 2, dtype=np.float32) * np.float32(-np.log(10000.0) / HD)).astype(np.float64)
    angle = div[:, None] * np.arange(T)
    sin, cos = np.sin(angle), np.cos(angle)
    table = np.stack([np.stack([sin, -cos], 1), np.stack([cos, sin], 1)])
    rel_tab = np.repeat(table.reshape(2, HD, 1, T), H, axis=2).reshape(2, C, T).transpose(1, 0, 2).astype(np.float32)
    key = np.stack([cos, sin], 1).reshape(HD, T).astype(np.float32)
    high = key.astype(bf)
    mid = (key - high.astype(np.float32)).astype(bf)
    low = (key - high.astype(np.float32) - mid.astype(np.float32)).astype(bf)
    k_rel = np.concatenate([(high, mid, low)[p] for p in K_PARTS] + [np.ones((2, T), bf)])

    ins = {"x": a(L0_attn_x), "weights": weights, "cols": cols, "rows": rows, "rel_tab": rel_tab, "k_rel": k_rel,
           "ident_f": np.eye(P, dtype=np.float32), "ident_b": np.eye(P, dtype=bf)}
    ins = {n: np.ascontiguousarray(v) for n, v in ins.items()}
    nc = bacc.Bacc("TRN2", target_bir_lowering=False, num_devices=1)
    aps = {n: nc.dram_tensor(n, v.shape, mybir.dt.from_np(v.dtype), kind="ExternalInput").ap() for n, v in ins.items()}
    out = nc.dram_tensor("out", (B, T, C), mybir.dt.float32, kind="ExternalOutput").ap()
    scratch = nc.dram_tensor("scratch", (2, 3, C, T), mybir.dt.bfloat16, kind="Internal").ap()
    build(nc, *(aps[n] for n in ("x", "weights", "cols", "rows", "rel_tab", "k_rel", "ident_f", "ident_b")), out, scratch)
    return run_bass_kernel_spmd(nc, [ins], core_ids=[0]).results[0]["out"]
```

```python
from contextlib import ExitStack

import numpy as np

import concourse.bass as bass
from concourse import mybir

B, T, C, H, HD = 8, 512, 128, 16, 8
P = 128
TB = T // P
G = H // 4
STEPS = G * TB
LEAD = 6
Q_PARTS = (0, 1, 2, 0, 1, 0)
K_PARTS = (0, 0, 0, 1, 1, 2)
NPROD = len(Q_PARTS)
KREL = NPROD * HD
KMAX = 2 * KREL
KROWS = KMAX + 2
VW = 32
RING = 16
EPS = 1e-5
SCALE = HD ** -0.5
W_Q, W_K, W_V, W_R, W_KF, W_VF, W_O = range(7)
C_G, C_B, C_BQ, C_BK, C_MUR, C_MUK, C_WS, C_WC = range(8)

PLAN = {
    0: [None, None, ("xnT", "next")],
    1: [("o3", "prev"), None, ("xaT", "next")],
    2: [("q", "next"), ("m1", "this"), None],
    3: [("k", "next"), None, ("onT", "prev")],
    4: [("v", "next"), None, ("out", "prev")],
    5: [("o0", "this"), None, ("r", "next")],
    6: [("kf", "next"), ("m2", "this"), None],
    7: [None, None, ("kv", "next")],
    9: [("o1", "this"), None, None],
    10: [None, ("m3", "this"), None],
    13: [("o2", "this"), None, None],
    14: [None, ("m0", "next"), None],
}


def plan(kind, unit, place):
    use = PLAN.get(unit, [None] * 3)[place]
    return None if use is None or use[1] == {"first": "prev", "middle": None, "last": "next"}[kind] else use


def bank(tile):
    return 1 if tile == 4 * STEPS - 1 else tile % 3


def since_bank(tile):
    back = 1
    while bank((tile - back) % (4 * STEPS)) != bank(tile):
        back += 1
    return back


def build(nc, x, weights, cols, rows, rel_tab, k_rel, ident, out, scratch):
    fp32, bf16, i32 = mybir.dt.float32, mybir.dt.bfloat16, mybir.dt.int32
    ALU, ACT, AX = mybir.AluOpType, mybir.ActivationFunctionType, mybir.AxisListType

    ctx = ExitStack()
    with ctx:
        def sb(name, shape, dt=fp32):
            return ctx.enter_context(nc.sbuf_tensor(name, shape, dt))

        def sem(name):
            return ctx.enter_context(nc.semaphore(name))

        w_sb = sb("w_sb", [P, 7, C])
        c_sb = sb("c_sb", [P, 8])
        rel_w = sb("rel_w", [P, 2])
        table_in = sb("table_in", [P, 1])
        mu_rest = sb("mu_rest", [P, 2])
        row_sb = sb("row_sb", [P, 2, C])
        idf = sb("idf", [P, P])
        tab = sb("tab", [P, 2, T])
        x_all = sb("x_all", [P, B, TB, C])
        stats = sb("stats", [P, B, TB, 6])
        moments = sb("moments", [P, B * TB, 2])
        lnw = sb("lnw", [P, 2, B * TB])
        lny = sb("lny", [P, 2, B * TB])
        lnt = sb("lnt", [P, 2, B * TB])
        xn_tok = sb("xn_tok", [P, TB, C])
        xa_tok = sb("xa_tok", [P, TB, C])
        xnT = sb("xnT", [P, 1 + T])
        xaT = sb("xaT", [P, T])
        rel_full = sb("rel_full", [P, T])
        rel_left = sb("rel_left", [P, T])
        rel_parts = sb("rel_parts", [P, 3, T], bf16)
        left = [sb(f"left_{n}", [P, T]) for n in "qk"]
        parts = [sb(f"parts_{n}", [P, 3, T], bf16) for n in "qk"]
        Q = sb("Q", [KROWS, H, T], bf16)
        K = sb("K", [KROWS, H, T], bf16)
        negmax = sb("negmax", [P, 2, 16])
        nm_rows = sb("nm_rows", [16, 2, 2, P], bf16)
        v_stage = sb("v_stage", [P, TB, C])
        V = sb("V", [P, TB, H, VW])
        probs = sb("probs", [P, RING, T])
        o_raw = sb("o_raw", [P, T])
        rsum = sb("rsum", [P, 2, TB, 4])
        o_n = sb("o_n", [P, TB, C])
        oT = sb("oT", [P, T])
        mix_a = sb("mix_a", [P, T])
        mix_b = sb("mix_b", [P, T])
        xrT = sb("xrT", [P, T])
        xkT = sb("xkT", [P, T])
        th = sb("th", [P, TB, C])
        gate = sb("gate", [P, TB, C])
        relu = sb("relu", [P, T])
        kact = sb("kact", [P, T])
        ffn = sb("ffn", [P, TB, C])
        xb = sb("xb", [P, TB, C])
        res_next = sb("res_next", [P, TB, C])
        res = sb("res", [P, TB, C])
        y_sb = sb("y_sb", [P, TB, C])

        max_ps = ctx.enter_context(nc.psum_tensor("max_ps", [P, 3, T], fp32))
        sc_ps = ctx.enter_context(nc.psum_tensor("sc_ps", [P, 3, T], fp32))
        av_ps = ctx.enter_context(nc.psum_tensor("av_ps", [P, T], fp32))
        sh_ps = ctx.enter_context(nc.psum_tensor("sh_ps", [P, T], fp32))
        sh_tok = sh_ps[:, :].rearrange("p (j c) -> p j c", j=TB)
        sh_heads = sh_ps[:, :].rearrange("p (j h w) -> p j h w", j=TB, w=VW)
        sh_m = sh_ps[0:16, 0:P]

        x_first_loaded = sem("x_first_loaded")
        x_rest_loaded = sem("x_rest_loaded")
        cols_loaded = sem("cols_loaded")
        weights_loaded = sem("weights_loaded")
        tables_loaded = sem("tables_loaded")
        rows_loaded = sem("rows_loaded")
        ident_loaded = sem("ident_loaded")
        krel_loaded = sem("krel_loaded")
        rel_written = sem("rel_written")
        qrel_loaded = sem("qrel_loaded")
        scratch_written = [sem(f"scratch_{n}_written") for n in "qk"]
        slab_loaded = [sem(f"slab{g}_loaded") for g in range(G)]
        m_loaded = [sem(f"m{g}_loaded") for g in range(G)]
        y_stored = sem("y_stored")
        max_tile = sem("max_tile")
        score_tile = sem("score_tile")
        av_step = sem("av_step")
        xnT_made = sem("xnT_made")
        xaT_made = sem("xaT_made")
        q_made = sem("q_made")
        k_made = sem("k_made")
        v_made = sem("v_made")
        r_made = sem("r_made")
        kf_made = sem("kf_made")
        kv_made = sem("kv_made")
        m_made = sem("m_made")
        o_made = sem("o_made")
        onT_made = sem("onT_made")
        out_made = sem("out_made")
        rows_maxed = sem("rows_maxed")
        probs_ready = sem("probs_ready")
        small_ready = sem("small_ready")
        zeros_ready = sem("zeros_ready")
        ln_chain = sem("ln_chain")
        xn_ready = sem("xn_ready")
        xa_ready = sem("xa_ready")
        xnT_ready = sem("xnT_ready")
        xaT_ready = sem("xaT_ready")
        high_ready = [sem(f"high_{n}_ready") for n in "qk"]
        left_ready = [sem(f"left_{n}_ready") for n in "qk"]
        mid_ready = [sem(f"mid_{n}_ready") for n in "qk"]
        parts_ready = [sem(f"parts_{n}_ready") for n in "qk"]
        rel_two = sem("rel_two")
        rel_chain = sem("rel_chain")
        rel_parts_ready = sem("rel_parts_ready")
        m_high = sem("m_high")
        m_low = sem("m_low")
        v_staged = sem("v_staged")
        v_ready = sem("v_ready")
        mix_chain = sem("mix_chain")
        xr_ready = sem("xr_ready")
        xk_ready = sem("xk_ready")
        th_ready = sem("th_ready")
        relu_ready = sem("relu_ready")
        gate_ready = sem("gate_ready")
        kact_ready = sem("kact_ready")
        xb_ready = sem("xb_ready")
        ffn_ready = sem("ffn_ready")
        res_next_ready = sem("res_next_ready")
        res_ready = sem("res_ready")
        o_raw_ready = sem("o_raw_ready")
        rsum_ready = sem("rsum_ready")
        o_n_ready = sem("o_n_ready")
        oT_ready = sem("oT_ready")
        y_ready = sem("y_ready")
        waited = sem("waited")

        block = ctx.enter_context(nc.Block())

        def bodies(eng, body):
            body("first", 0)
            with eng.Fori(1, B - 1) as b:
                body("middle", b)
            body("last", B - 1)

        def chain(eng, sem_, base):
            done = [base]

            def link(ins):
                ins.then_inc(sem_, 1)
                done[0] = done[0] + 1
                eng.wait_ge(sem_, done[0])
            return link

        def positive(v):
            return not isinstance(v, int) or v > 0

        def settle(eng):
            eng.sem_inc(waited, 1)

        @block.sync
        def _(sp):
            def write_scratch(n):
                sp.dma_start(scratch[n].rearrange("a p t -> p a t"), parts[n][:, :, :]).then_inc(scratch_written[n], 16)

            by_dim = scratch.rearrange("n a (d h) t -> n a d h t", h=H)

            def load_q(g):
                hs = slice(4 * g, 4 * g + 4)
                for row, n in ((0, 3), (3, 2), (5, 1)):
                    sp.dma_start(Q[row * HD:(row + n) * HD, hs, :],
                                 by_dim[0, 0:n, :, hs, :].rearrange("a d h t -> (a d) h t")).then_inc(slab_loaded[g], 16)

            def load_k(g):
                hs = slice(4 * g, 4 * g + 4)
                for part, (row, n) in enumerate(((0, 3), (3, 2), (5, 1))):
                    sp.dma_start(K[row * HD:(row + n) * HD, hs, :],
                                 by_dim[1, part:part + 1, :, hs, :].to_broadcast([n, HD, 4, T])).then_inc(slab_loaded[g], 16)

            def load_m(g, b):
                after = (b - 1) * 4 * STEPS + 16 * (g + 1)
                if positive(after):
                    sp.wait_ge(score_tile, after)
                    settle(sp)
                for p, ready in enumerate((m_high, m_low)):
                    sp.wait_ge(ready, 4 * b + g + 1)
                    settle(sp)
                    sp.dma_start(Q[KMAX + p:KMAX + p + 1, 4 * g:4 * g + 4, :],
                                 nm_rows[:, g % 2, p, :]).then_inc(m_loaded[g], 16)

            def slab(g, b):
                after = (b - 1) * 4 * STEPS + 16 * (g + 1)
                if positive(after):
                    sp.wait_ge(score_tile, after)
                    settle(sp)
                load_q(g)
                load_k(g)

            def store(b):
                sp.wait_ge(y_ready, b + 1)
                settle(sp)
                sp.dma_start(out[bass.ds(b, 1)].rearrange("o (j p) c -> p (o j) c", p=P), y_sb[:, :, :]).then_inc(y_stored, 16)

            sp.dma_start(x_all[:, 0], x[0].rearrange("(j p) c -> p j c", p=P)).then_inc(x_first_loaded, 16)
            sp.dma_start(c_sb[:, :], cols).then_inc(cols_loaded, 16)
            sp.dma_start(tab[:, :, :], rel_tab).then_inc(tables_loaded, 16)
            sp.dma_start(idf[:, :], ident).then_inc(ident_loaded, 16)
            sp.dma_start(w_sb[:, :, :], weights).then_inc(weights_loaded, 16)
            sp.dma_start(row_sb[:, :, :], rows.partition_broadcast(P)).then_inc(rows_loaded, 16)
            sp.dma_start(K[KREL:KROWS, :, :], k_rel[:, None, :].to_broadcast([KROWS - KREL, H, T])).then_inc(krel_loaded, 16)
            sp.dma_start(x_all[:, 1:], x[1:].rearrange("b (j p) c -> p b j c", p=P)).then_inc(x_rest_loaded, 16)
            sp.wait_ge(rel_parts_ready, 1)
            sp.dma_start(scratch[2].rearrange("a p t -> p a t"), rel_parts[:, :, :]).then_inc(rel_written, 16)
            sp.wait_ge(rel_written, 16)
            for row, n in ((0, 3), (3, 2), (5, 1)):
                sp.dma_start(Q[KREL + row * HD:KREL + (row + n) * HD, :, :],
                             by_dim[2, 0:n].rearrange("a d h t -> (a d) h t")).then_inc(qrel_loaded, 16)
            sp.wait_ge(parts_ready[0], 1)
            write_scratch(0)
            sp.wait_ge(scratch_written[0], 16)
            load_q(0)
            sp.wait_ge(parts_ready[1], 1)
            write_scratch(1)
            sp.wait_ge(scratch_written[1], 16)
            load_k(0)
            for g in range(1, G):
                load_q(g)
                load_k(g)
            load_m(0, 0)

            def body(kind, b):
                load_m(1, b)
                if kind == "last":
                    store(b - 1)
                    load_m(2, b)
                    load_m(3, b)
                    return
                for g in range(G):
                    sp.wait_ge(slab_loaded[g], 6 * 16 * (b + 1))
                    settle(sp)
                for n in range(2):
                    sp.wait_ge(parts_ready[n], b + 2)
                    settle(sp)
                    write_scratch(n)
                if kind != "first":
                    store(b - 1)
                for n in range(2):
                    sp.wait_ge(scratch_written[n], 16 * (b + 2))
                    settle(sp)
                slab(0, b + 1)
                load_m(2, b)
                slab(1, b + 1)
                load_m(3, b)
                slab(2, b + 1)
                load_m(0, b + 1)
                slab(3, b + 1)

            bodies(sp, body)
            store(B - 1)
            sp.wait_ge(y_stored, 16 * B)

        @block.tensor
        def _(pe):
            last_use = []

            def take_bank(name, b):
                if last_use:
                    before, of = last_use
                    count = of + 1
                    if before[0] == "m":
                        done, count = m_low, 4 * of + int(before[1]) + 1
                    elif before[0] == "o" and before[1].isdigit():
                        done, count = o_n_ready, 4 * of + int(before[1]) + 1
                    else:
                        done = {"xnT": xnT_ready, "xaT": xaT_ready, "q": left_ready[0], "k": left_ready[1],
                                "v": v_staged, "r": th_ready, "kf": relu_ready, "kv": ffn_ready,
                                "onT": oT_ready, "out": y_ready}[before]
                    pe.wait_ge(done, count)
                last_use[:] = name, b

            def transposes(src, made):
                for j in range(TB):
                    last = nc.tensor.transpose(sh_ps[:, j * P:(j + 1) * P], src[:, j * P:(j + 1) * P], idf[:, :])
                last.then_inc(made, 1)

            def by_token(lhs, w, made):
                for j in range(TB):
                    last = nc.tensor.matmul(sh_ps[:, j * P:(j + 1) * P], lhs[:, j * P:(j + 1) * P],
                                            w_sb[:, w, :], start=True, stop=True)
                last.then_inc(made, 1)

            def by_channel(w, rhs, made):
                nc.tensor.matmul(sh_ps[:, :], w_sb[:, w, :], rhs[:, :], start=True, stop=True).then_inc(made, 1)

            flat = "p j c -> p (j c)"

            def use(name, b):
                take_bank(name, b)
                if name == "xnT":
                    pe.wait_ge(xn_ready, 4 * (b + 1))
                    transposes(xn_tok[:, :, :].rearrange(flat), xnT_made)
                elif name == "xaT":
                    pe.wait_ge(xa_ready, 4 * (b + 1))
                    transposes(xa_tok[:, :, :].rearrange(flat), xaT_made)
                elif name == "q":
                    pe.wait_ge(xaT_ready, b + 1)
                    by_channel(W_Q, xaT, q_made)
                elif name == "k":
                    by_channel(W_K, xaT, k_made)
                elif name == "v":
                    by_token(xaT, W_V, v_made)
                elif name == "r":
                    pe.wait_ge(xr_ready, b + 1)
                    by_token(xrT, W_R, r_made)
                elif name == "kf":
                    pe.wait_ge(xk_ready, b + 1)
                    by_channel(W_KF, xkT, kf_made)
                elif name == "kv":
                    pe.wait_ge(kact_ready, b + 1)
                    by_token(kact, W_VF, kv_made)
                elif name[0] == "m":
                    g = int(name[1])
                    pe.wait_ge(rows_maxed, b * 4 * STEPS + 16 * (g + 1))
                    nc.tensor.transpose(sh_m, negmax[:, g % 2, :], idf[:, :]).then_inc(m_made, 1)
                elif name == "onT":
                    pe.wait_ge(o_n_ready, 4 * (b + 1))
                    transposes(o_n[:, :, :].rearrange(flat), onT_made)
                elif name == "out":
                    pe.wait_ge(oT_ready, b + 1)
                    by_token(oT, W_O, out_made)
                else:
                    pe.wait_ge(o_raw_ready, 4 * b + int(name[1]) + 1)
                    transposes(o_raw, o_made)

            def max_tile_of(pos, b, i):
                g, head = pos // 4, pos
                n = b * 4 * STEPS + 4 * pos + i
                if pos % 4 == 0 and i == 0:
                    pe.wait_ge(slab_loaded[g], 6 * 16 * (b + 1))
                free = n - since_bank(4 * pos + i) + 1
                if positive(free):
                    pe.wait_ge(rows_maxed, free)
                nc.tensor.matmul(max_ps[:, bank(4 * pos + i), :], Q[0:KMAX, head, i * P:(i + 1) * P], K[0:KMAX, head, :],
                                 start=True, stop=True).then_inc(max_tile, 1)

            def score_tile_of(s, b, i):
                g, kt = s // 4, s % 4
                n = b * 4 * STEPS + 4 * s + i
                if kt == 0 and i == 0:
                    pe.wait_ge(m_loaded[g], 32 * (b + 1))
                free = n - since_bank(4 * s + i) + 1
                if positive(free):
                    pe.wait_ge(probs_ready, free)
                head = 4 * g + i
                nc.tensor.matmul(sc_ps[:, bank(4 * s + i), :], K[:, head, kt * P:(kt + 1) * P], Q[:, head, :],
                                 start=True, stop=True).then_inc(score_tile, 1)

            def av(s, b):
                g, kt = s // 4, s % 4
                pe.wait_ge(probs_ready, b * 4 * STEPS + 4 * s + 4)
                if kt == 0:
                    pe.wait_ge(v_ready, 4 * b + g + 1)
                    if positive(4 * b + g):
                        pe.wait_ge(o_raw_ready, 4 * b + g)
                for i in range(4):
                    last = nc.tensor.matmul(av_ps[VW * i:VW * (i + 1), :], V[:, kt, 4 * g + i, :],
                                            probs[:, (4 * s + i) % RING, :], start=kt == 0, stop=kt == TB - 1)
                last.then_inc(av_step, 1)

            pe.wait_ge(ident_loaded, 16)
            use("xaT", 0)
            pe.wait_ge(weights_loaded, 16)
            for name in ("q", "k", "xnT"):
                use(name, 0)
            pe.wait_ge(krel_loaded, 16)
            pe.wait_ge(qrel_loaded, 48)
            for pos in range(LEAD):
                for i in range(4):
                    max_tile_of(pos, 0, i)
                    if (pos, i) == (4, 1):
                        use("m0", 0)
                if pos < 4:
                    use(("v", "r", "kf", "kv")[pos], 0)

            def body(kind, b):
                of = {"prev": b - 1, "this": b, "next": b + 1}
                last_use[:] = "m0", b
                for s in range(STEPS):
                    for i in range(4):
                        ahead = s + LEAD
                        if ahead < STEPS:
                            max_tile_of(ahead, b, i)
                        elif kind != "last":
                            max_tile_of(ahead - STEPS, b + 1, i)
                        score_tile_of(s, b, i)
                        if i == 1 and s > 0:
                            av(s - 1, b)
                        elif i == 1 and kind != "first":
                            av(STEPS - 1, b - 1)
                        if i < 3 and plan(kind, s, i) is not None:
                            name, whose = plan(kind, s, i)
                            use(name, of[whose])

            bodies(pe, body)
            av(STEPS - 1, B - 1)
            for name in ("o3", "onT", "out"):
                use(name, B - 1)

        @block.scalar
        def _(act):
            def exp_tile(s, b, i):
                n = b * 4 * STEPS + 4 * s + i
                if i == 0:
                    before = b * STEPS + s - RING // 4 + 1
                    if positive(before):
                        act.wait_ge(av_step, before)
                act.wait_ge(score_tile, n + 1)
                nc.scalar.activation(probs[:, (4 * s + i) % RING, :], sc_ps[:, bank(4 * s + i), :], ACT.Exp,
                                     scale=SCALE).then_inc(probs_ready, 1)

            def read_av(s, b):
                act.wait_ge(av_step, b * STEPS + s + 1)
                n = 4 * b + s // 4
                if positive(n):
                    act.wait_ge(o_made, n)
                nc.scalar.copy(o_raw[:, :], av_ps[:, :]).then_inc(o_raw_ready, 1)

            def read_out(name, b):
                if name == "xnT":
                    act.wait_ge(xnT_made, b + 1)
                    if positive(b):
                        act.wait_ge(xk_ready, b)
                    ins, done = nc.scalar.copy(xnT[:, 1:], sh_ps[:, :]), xnT_ready
                elif name == "xaT":
                    act.wait_ge(xaT_made, b + 1)
                    if positive(b):
                        act.wait_ge(v_made, b)
                    ins, done = nc.scalar.activation(xaT[:, :], sh_ps[:, :], ACT.Identity, bias=c_sb[:, C_B:C_B + 1],
                                                     scale=c_sb[:, C_G:C_G + 1]), xaT_ready
                elif name in ("q", "k"):
                    n = "qk".index(name)
                    act.wait_ge((q_made, k_made)[n], b + 1)
                    if positive(b):
                        act.wait_ge(scratch_written[n], 16 * b)
                    bias = (C_BQ, C_BK)[n]
                    ins, done = nc.scalar.activation(parts[n][:, 0, :], sh_ps[:, :], ACT.Identity,
                                                     bias=c_sb[:, bias:bias + 1]), high_ready[n]
                elif name == "r":
                    act.wait_ge(r_made, b + 1)
                    if positive(b):
                        act.wait_ge(gate_ready, b)
                    ins, done = nc.scalar.activation(th[:, :, :], sh_tok, ACT.Tanh, scale=0.5), th_ready
                elif name == "kf":
                    act.wait_ge(kf_made, b + 1)
                    if positive(b):
                        act.wait_ge(kact_ready, b)
                    ins, done = nc.scalar.activation(relu[:, :], sh_ps[:, :], ACT.Relu), relu_ready
                elif name == "onT":
                    act.wait_ge(onT_made, b + 1)
                    if positive(b):
                        act.wait_ge(out_made, b)
                    ins, done = nc.scalar.copy(oT[:, :], sh_ps[:, :]), oT_ready
                elif name[0] == "m":
                    g = int(name[1])
                    act.wait_ge(m_made, 4 * b + g + 1)
                    before = b if g >= 2 else b - 1
                    if positive(before + (g >= 2)):
                        act.wait_ge(m_loaded[(g + 2) % 4], 32 * (before + 1))
                    ins, done = nc.scalar.copy(nm_rows[:, g % 2, 0, :], sh_m), m_high
                else:
                    return
                ins.then_inc(done, 1)

            act.wait_ge(cols_loaded, 16)
            nc.scalar.activation(table_in[:, :], c_sb[:, 0:1], ACT.Exp)
            for name in ("xaT", "q", "k", "xnT", "r", "kf", "m0"):
                read_out(name, 0)

            def body(kind, b):
                of = {"prev": b - 1, "this": b, "next": b + 1}
                for s in range(STEPS):
                    for i in range(4):
                        exp_tile(s, b, i)
                        if i == 1 and s % 4 == 0 and s > 0:
                            read_av(s - 1, b)
                        elif i == 1 and s == 0 and kind != "first":
                            read_av(STEPS - 1, b - 1)
                        if i < 3 and plan(kind, s, i) is not None:
                            name, whose = plan(kind, s, i)
                            read_out(name, of[whose])

            bodies(act, body)
            read_av(STEPS - 1, B - 1)
            read_out("onT", B - 1)

        @block.vector
        def _(dve):
            ln = chain(dve, ln_chain, 0)

            def statistics(bs):
                for b in bs:
                    for j in range(TB):
                        last = nc.vector.bn_stats(stats[:, b, j, :], x_all[:, b, j, :])
                ln(last)
                n0, n1 = bs[0] * TB, (bs[-1] + 1) * TB
                for b in bs:
                    for j in range(TB):
                        last = nc.vector.bn_aggr(moments[:, b * TB + j, :], stats[:, b, j, :])
                ln(last)
                var = moments[:, n0:n1, 1]
                w, y, t = (a[:, :, n0:n1] for a in (lnw, lny, lnt))
                nc.vector.tensor_scalar(lnw[:, 0, n0:n1], var, EPS, None, ALU.add)
                ln(nc.vector.tensor_scalar(lnw[:, 1, n0:n1], var, 1.0 + EPS, EPS * EPS, ALU.mult, ALU.add))
                ln(nc.vector.tensor_scalar(y.bitcast(i32), w.bitcast(i32), -0.5, float(0x5f3759df), ALU.mult, ALU.add))
                for _ in range(4):
                    ln(nc.vector.scalar_tensor_tensor(t, y, -0.5, y, ALU.mult, ALU.mult))
                    ln(nc.vector.tensor_tensor(t, t, w, ALU.mult))
                    ln(nc.vector.scalar_tensor_tensor(y, t, 1.5, y, ALU.add, ALU.mult))

            def normalise(b, which):
                if positive(b):
                    dve.wait_ge((xnT_made, xaT_made)[which], b)
                dst = (xn_tok, xa_tok)[which]
                for j in range(TB):
                    n = b * TB + j
                    nc.vector.tensor_scalar(dst[:, j, :], x_all[:, bass.ds(b, 1), j, :].rearrange("p o c -> p (o c)"),
                                            moments[:, bass.ds(n, 1), 0], lny[:, which, bass.ds(n, 1)],
                                            ALU.subtract, ALU.mult).then_inc((xn_ready, xa_ready)[which], 1)

            def reduce_tile(pos, b, i):
                n = b * 4 * STEPS + 4 * pos + i
                g = pos // 4
                if pos % 4 == 0 and i == 0:
                    before = 4 * b + g - 1
                    if positive(before):
                        dve.wait_ge(m_made, before)
                dve.wait_ge(max_tile, n + 1)
                col = 4 * (pos % 4) + i
                nc.vector.tensor_reduce(negmax[:, g % 2, col:col + 1], max_ps[:, bank(4 * pos + i), :], AX.X, ALU.max,
                                        negate=True).then_inc(rows_maxed, 1)

            def read_out(name, b):
                if name in ("q", "k"):
                    n = "qk".index(name)
                    dve.wait_ge(high_ready[n], b + 1)
                    if positive(b):
                        dve.wait_ge(parts_ready[n], b)
                    bias = (C_BQ, C_BK)[n]
                    ins = nc.vector.scalar_tensor_tensor(left[n][:, :], sh_ps[:, :], c_sb[:, bias:bias + 1],
                                                         parts[n][:, 0, :], ALU.add, ALU.subtract)
                    ins.then_inc(left_ready[n], 1)
                elif name == "v":
                    dve.wait_ge(v_made, b + 1)
                    if positive(4 * b):
                        dve.wait_ge(v_ready, 4 * b)
                    ins = nc.vector.tensor_tensor(v_stage[:, :, :], sh_tok,
                                                  row_sb[:, 0:1, :].to_broadcast([P, TB, C]), ALU.add)
                    ins.then_inc(v_staged, 1)
                elif name == "kv":
                    dve.wait_ge(kv_made, b + 1)
                    dve.wait_ge(gate_ready, b + 1)
                    if positive(b):
                        dve.wait_ge(res_next_ready, b)
                    ins = nc.vector.tensor_tensor(ffn[:, :, :], sh_tok, gate[:, :, :], ALU.mult)
                    ins.then_inc(ffn_ready, 1)
                elif name == "out":
                    dve.wait_ge(out_made, b + 1)
                    dve.wait_ge(res_ready, b + 1)
                    if positive(b):
                        dve.wait_ge(y_stored, 16 * b)
                    ins = nc.vector.tensor_tensor(y_sb[:, :, :], sh_tok, res[:, :, :], ALU.add)
                    ins.then_inc(y_ready, 1)
                elif name[0] == "m":
                    g = int(name[1])
                    dve.wait_ge(m_high, 4 * b + g + 1)
                    before = b if g >= 2 else b - 1
                    if positive(before + (g >= 2)):
                        dve.wait_ge(m_loaded[(g + 2) % 4], 32 * (before + 1))
                    nc.vector.tensor_tensor(nm_rows[:, g % 2, 1, :], sh_m, nm_rows[:, g % 2, 0, :],
                                            ALU.subtract).then_inc(m_low, 1)
                    return
                elif name[0] == "o" and name != "onT":
                    g = int(name[1])
                    dve.wait_ge(o_made, 4 * b + g + 1)
                    nc.vector.reciprocal(rsum[:, g % 2], sh_heads[:, :, :, HD]).then_inc(rsum_ready, 1)
                    if g == 0 and positive(b):
                        dve.wait_ge(onT_made, b)
                    dve.wait_ge(rsum_ready, 4 * b + g + 1)
                    heads = o_n[:, :, :].rearrange("p j (h d) -> p j h d", d=HD)[:, :, 4 * g:4 * g + 4, :]
                    ins = nc.vector.tensor_tensor(heads, sh_heads[:, :, :, 0:HD],
                                                  rsum[:, g % 2][:, :, :, None].to_broadcast([P, TB, 4, HD]), ALU.mult)
                    ins.then_inc(o_n_ready, 1)

            dve.wait_ge(x_first_loaded, 16)
            dve.wait_ge(cols_loaded, 16)
            nc.vector.tensor_scalar(rel_w[:, :], c_sb[:, C_WS:C_WC + 1], 1.0 / SCALE, None, ALU.mult).then_inc(small_ready, 1)
            for n, c in enumerate((C_MUR, C_MUK)):
                nc.vector.tensor_scalar(mu_rest[:, n:n + 1], c_sb[:, c:c + 1], -1.0, 1.0, ALU.mult,
                                        ALU.add).then_inc(small_ready, 1)
            statistics([0])
            normalise(0, 1)
            normalise(0, 0)
            for n in range(2):
                read_out("qk"[n], 0)
                dve.wait_ge(left_ready[n], 1)
                nc.vector.tensor_copy(parts[n][:, 1, :], left[n][:, :]).then_inc(mid_ready[n], 1)
                dve.wait_ge(mid_ready[n], 1)
                nc.vector.tensor_tensor(parts[n][:, 2, :], left[n][:, :], parts[n][:, 1, :],
                                        ALU.subtract).then_inc(parts_ready[n], 1)
            dve.wait_ge(x_rest_loaded, 16)
            statistics(list(range(1, B)))
            for pos in range(LEAD):
                for i in range(4):
                    reduce_tile(pos, 0, i)
                    if (pos, i) == (4, 1):
                        read_out("m0", 0)
                if pos == 0:
                    dve.wait_ge(rows_loaded, 16)
                    read_out("v", 0)
                elif pos == 3:
                    read_out("kv", 0)

            def body(kind, b):
                of = {"prev": b - 1, "this": b, "next": b + 1}
                for s in range(STEPS):
                    for i in range(4):
                        ahead = s + LEAD
                        if ahead < STEPS:
                            reduce_tile(ahead, b, i)
                        elif kind != "last":
                            reduce_tile(ahead - STEPS, b + 1, i)
                        if i < 3 and plan(kind, s, i) is not None:
                            name, whose = plan(kind, s, i)
                            read_out(name, of[whose])
                        if kind != "last" and s == 0 and i in (0, 2):
                            normalise(b + 1, i // 2)

            bodies(dve, body)
            read_out("o3", B - 1)
            read_out("out", B - 1)

        @block.gpsimd
        def _(pool):
            def cast(dst, src):
                settle(pool)
                return nc.gpsimd.tensor_scalar(dst, src, 1.0, 0.0, ALU.mult, ALU.add)

            def split(n, b):
                pool.wait_ge(left_ready[n], b + 1)
                r, p = left[n], parts[n]
                cast(p[:, 1, :], r[:, :]).then_inc(mid_ready[n], 1)
                pool.wait_ge(mid_ready[n], b + 1)
                nc.gpsimd.tensor_tensor(p[:, 2, :], r[:, :], p[:, 1, :], ALU.subtract).then_inc(parts_ready[n], 1)

            def place_v(g, b):
                pool.wait_ge(v_staged, b + 1)
                after = (b - 1) * STEPS + 4 * (g + 1)
                if positive(after):
                    pool.wait_ge(av_step, after)
                settle(pool)
                for j in range(TB):
                    last = cast(V[:, j, 4 * g:4 * g + 4, 0:HD],
                                v_stage[:, j, 4 * HD * g:4 * HD * (g + 1)].rearrange("p (h d) -> p h d", d=HD))
                last.then_inc(v_ready, 1)

            def mix(b):
                pool.wait_ge(xnT_ready, b + 1)
                link = chain(pool, mix_chain, 2 * b)
                for n, (mu, dst, made, ready) in enumerate(((C_MUR, xrT, r_made, xr_ready), (C_MUK, xkT, kf_made, xk_ready))):
                    if n == 1:
                        pool.wait_ge(xr_ready, b + 1)
                    elif positive(b):
                        pool.wait_ge(xk_ready, b)
                    settle(pool)
                    nc.gpsimd.tensor_scalar(mix_a[:, :], xnT[:, 1:], c_sb[:, mu:mu + 1], 0.0, ALU.mult, ALU.add)
                    link(nc.gpsimd.tensor_scalar(mix_b[:, :], xnT[:, 0:T], mu_rest[:, n:n + 1], 0.0, ALU.mult, ALU.add))
                    if positive(b):
                        pool.wait_ge(made, b)
                    nc.gpsimd.tensor_tensor(dst[:, :], mix_a[:, :], mix_b[:, :], ALU.add).then_inc(ready, 1)

            def x_and_bias(b):
                if positive(b):
                    pool.wait_ge(res_next_ready, b)
                nc.gpsimd.tensor_tensor(xb[:, :, :], x_all[:, bass.ds(b, 1)].rearrange("p o j c -> p (o j) c"),
                                        row_sb[:, 1:2, :].to_broadcast([P, TB, C]), ALU.add).then_inc(xb_ready, 1)

            def gate_of(b):
                pool.wait_ge(th_ready, b + 1)
                if positive(b):
                    pool.wait_ge(ffn_ready, b)
                settle(pool)
                nc.gpsimd.tensor_scalar(gate[:, :, :], th[:, :, :], 0.5, 0.5, ALU.mult, ALU.add).then_inc(gate_ready, 1)

            def square(b):
                pool.wait_ge(relu_ready, b + 1)
                if positive(b):
                    pool.wait_ge(kv_made, b)
                nc.gpsimd.tensor_tensor(kact[:, :], relu[:, :], relu[:, :], ALU.mult).then_inc(kact_ready, 1)

            def residual(b):
                pool.wait_ge(ffn_ready, b + 1)
                pool.wait_ge(xb_ready, b + 1)
                if positive(b):
                    pool.wait_ge(res_ready, b)
                nc.gpsimd.tensor_tensor(res_next[:, :, :], ffn[:, :, :], xb[:, :, :], ALU.add).then_inc(res_next_ready, 1)

            def hand_over(b):
                pool.wait_ge(res_next_ready, b + 1)
                if positive(b):
                    pool.wait_ge(y_ready, b)
                settle(pool)
                cast(res[:, :, :], res_next[:, :, :]).then_inc(res_ready, 1)

            nc.gpsimd.memset(xnT[:, 0:1], 0.0).then_inc(zeros_ready, 1)
            nc.gpsimd.memset(V[:, :, :, HD:VW], 0.0).then_inc(zeros_ready, 1)
            pool.wait_ge(zeros_ready, 2)
            nc.gpsimd.memset(V[:, :, :, HD:HD + 1], 1.0).then_inc(zeros_ready, 1)
            pool.wait_ge(zeros_ready, 3)
            pool.wait_ge(small_ready, 3)
            pool.wait_ge(tables_loaded, 16)
            rel = chain(pool, rel_chain, 0)
            nc.gpsimd.tensor_scalar(rel_full[:, :], tab[:, 0, :], rel_w[:, 0:1], 0.0, ALU.mult, ALU.add)
            nc.gpsimd.tensor_scalar(rel_left[:, :], tab[:, 1, :], rel_w[:, 1:2], 0.0, ALU.mult, ALU.add).then_inc(rel_two, 1)
            pool.wait_ge(rel_two, 1)
            rel(nc.gpsimd.tensor_tensor(rel_full[:, :], rel_full[:, :], rel_left[:, :], ALU.add))
            rel(cast(rel_parts[:, 0, :], rel_full[:, :]))
            rel(nc.gpsimd.tensor_tensor(rel_left[:, :], rel_full[:, :], rel_parts[:, 0, :], ALU.subtract))
            rel(cast(rel_parts[:, 1, :], rel_left[:, :]))
            nc.gpsimd.tensor_tensor(rel_parts[:, 2, :], rel_left[:, :], rel_parts[:, 1, :],
                                    ALU.subtract).then_inc(rel_parts_ready, 1)
            mix(0)
            pool.wait_ge(rows_loaded, 16)
            for g in range(G):
                place_v(g, 0)
            gate_of(0)
            square(0)
            x_and_bias(0)
            residual(0)

            def body(kind, b):
                if kind != "first":
                    place_v(3, b)
                if kind != "last":
                    mix(b + 1)
                    split(0, b + 1)
                    split(1, b + 1)
                hand_over(b)
                if kind != "last":
                    place_v(0, b + 1)
                    gate_of(b + 1)
                    square(b + 1)
                    x_and_bias(b + 1)
                    residual(b + 1)
                    place_v(1, b + 1)
                    place_v(2, b + 1)

            bodies(pool, body)


def kernel(L0_attn_x, L0_attn_ln_g, L0_attn_ln_b, L0_attn_w_qkv, L0_attn_b_qkv, L0_attn_w_rel, L0_attn_w_out,
           L0_attn_b_out, L0_ffn_W_r, L0_ffn_W_k, L0_ffn_W_v, L0_ffn_mu_r, L0_ffn_mu_k):
    import ml_dtypes

    import concourse.bacc as bacc
    from concourse.bass_utils import run_bass_kernel_spmd

    bf = ml_dtypes.bfloat16
    a = np.asarray
    w = a(L0_attn_w_qkv).reshape(C, 3, H, HD)
    bias = a(L0_attn_b_qkv).reshape(3, H, HD)
    dim_major = lambda m: np.swapaxes(m, -1, -2).reshape(*m.shape[:-2], C)
    weights = np.stack([dim_major(w[:, 0]), dim_major(w[:, 1]), w[:, 2].reshape(C, C), a(L0_ffn_W_r).T,
                        a(L0_ffn_W_k).T, a(L0_ffn_W_v).T, a(L0_attn_w_out)], axis=1)
    rel = np.repeat(a(L0_attn_w_rel).reshape(HD // 2, 2, H), 2, axis=0)
    cols = np.stack([a(L0_attn_ln_g), a(L0_attn_ln_b), dim_major(bias[0]), dim_major(bias[1]), a(L0_ffn_mu_r),
                     a(L0_ffn_mu_k), rel[:, 0].reshape(C), rel[:, 1].reshape(C)], axis=1)
    rows = np.stack([bias[2].reshape(C), a(L0_attn_b_out)])

    div = np.exp(np.arange(0, HD, 2, dtype=np.float32) * np.float32(-np.log(10000.0) / HD)).astype(np.float64)
    angle = div[:, None] * np.arange(T)
    sin, cos = np.sin(angle), np.cos(angle)
    table = np.stack([np.stack([sin, -cos], 1), np.stack([cos, sin], 1)])
    rel_tab = np.repeat(table.reshape(2, HD, 1, T), H, axis=2).reshape(2, C, T).transpose(1, 0, 2).astype(np.float32)
    key = np.stack([cos, sin], 1).reshape(HD, T).astype(np.float32)
    high = key.astype(bf)
    mid = (key - high.astype(np.float32)).astype(bf)
    low = (key - high.astype(np.float32) - mid.astype(np.float32)).astype(bf)
    k_rel = np.concatenate([(high, mid, low)[p] for p in K_PARTS] + [np.ones((2, T), bf)])

    ins = {"x": a(L0_attn_x), "weights": weights, "cols": cols, "rows": rows, "rel_tab": rel_tab, "k_rel": k_rel,
           "ident": np.eye(P, dtype=np.float32)}
    ins = {n: np.ascontiguousarray(v) for n, v in ins.items()}
    nc = bacc.Bacc("TRN2", target_bir_lowering=False, num_devices=1)
    aps = {n: nc.dram_tensor(n, v.shape, mybir.dt.from_np(v.dtype), kind="ExternalInput").ap() for n, v in ins.items()}
    out = nc.dram_tensor("out", (B, T, C), mybir.dt.float32, kind="ExternalOutput").ap()
    scratch = nc.dram_tensor("scratch", (3, 3, C, T), mybir.dt.bfloat16, kind="Internal").ap()
    build(nc, *(aps[n] for n in ("x", "weights", "cols", "rows", "rel_tab", "k_rel", "ident")), out, scratch)
    return run_bass_kernel_spmd(nc, [ins], core_ids=[0]).results[0]["out"]
```

```python
from contextlib import ExitStack

import numpy as np

import concourse.bass as bass
from concourse import mybir

B, T, C, H, HD = 8, 512, 128, 16, 8
P = 128
TB = T // P
G = H // 4
STEPS = G * TB
LEAD = 6
Q_PARTS = (0, 1, 2, 0, 1, 0)
K_PARTS = (0, 0, 0, 1, 1, 2)
NPROD = len(Q_PARTS)
KREL = NPROD * HD
KMAX = 2 * KREL
KROWS = KMAX + 2
VW = 32
WARM_UP = 10
AV_AFTER = {"first": 2, "middle": 1, "last": 2}
RING = 16
EARLY = 5
EPS = 1e-5
SCALE = HD ** -0.5
W_Q, W_K, W_V, W_R, W_KF, W_VF, W_O = range(7)
C_G, C_B, C_BQ, C_BK, C_MUR, C_MUK, C_WS, C_WC = range(8)

PLAN = {
    0: [("xaT", "next"), ("xnT", "next"), None],
    1: [("o3", "prev"), None, ("q", "next")],
    2: [None, ("m1", "this"), None],
    3: [("k", "next"), None, None],
    4: [("onT", "prev"), None, None],
    5: [("out", "prev"), ("o0", "this"), None],
    6: [("r", "next"), ("m2", "this"), None],
    7: [None, ("kf", "next"), None],
    8: [("v", "next"), None, None],
    9: [("o1", "this"), None, None],
    10: [("kv", "next"), ("m3", "this"), None],
    13: [("o2", "this"), None, None],
    14: [None, ("m0", "next"), None],
}


def plan(kind, unit, place):
    use = PLAN.get(unit, [None] * 3)[place]
    return None if use is None or use[1] == {"first": "prev", "middle": None, "last": "next"}[kind] else use


def bank(tile):
    return 1 if tile == 4 * STEPS - 1 else tile % 3


def since_bank(tile):
    back = 1
    while bank((tile - back) % (4 * STEPS)) != bank(tile):
        back += 1
    return back


def build(nc, x, weights, cols, rows, rel_tab, k_rel, ident, out, scratch):
    fp32, bf16, i32 = mybir.dt.float32, mybir.dt.bfloat16, mybir.dt.int32
    ALU, ACT, AX = mybir.AluOpType, mybir.ActivationFunctionType, mybir.AxisListType

    ctx = ExitStack()
    with ctx:
        def sb(name, shape, dt=fp32):
            return ctx.enter_context(nc.sbuf_tensor(name, shape, dt))

        def sem(name):
            return ctx.enter_context(nc.semaphore(name))

        w_sb = sb("w_sb", [P, 7, C])
        c_sb = sb("c_sb", [P, 8])
        rel_w = sb("rel_w", [P, 2])
        table_in = sb("table_in", [P, 1])
        mu_rest = sb("mu_rest", [P, 2])
        row_sb = sb("row_sb", [P, 2, C])
        idf = sb("idf", [P, P])
        tab = sb("tab", [P, 2, T])
        x_all = sb("x_all", [P, B, TB, C])
        stats = sb("stats", [P, B, TB, 6])
        moments = sb("moments", [P, B * TB, 2])
        lnw = sb("lnw", [P, 2, B * TB])
        lny = sb("lny", [P, 2, B * TB])
        lnt = sb("lnt", [P, 2, B * TB])
        x_less_mean = sb("x_less_mean", [P, TB, C])
        xn_tok = sb("xn_tok", [P, TB, C])
        xa_tok = sb("xa_tok", [P, TB, C])
        xnT = sb("xnT", [P, 1 + T])
        xaT = sb("xaT", [P, T])
        rel_full = sb("rel_full", [P, T])
        rel_left = sb("rel_left", [P, T])
        rel_parts = sb("rel_parts", [P, 3, T], bf16)
        left = [sb(f"left_{n}", [P, T]) for n in "qk"]
        parts = [sb(f"parts_{n}", [P, 3, T], bf16) for n in "qk"]
        Q = sb("Q", [KROWS, H, T], bf16)
        K = sb("K", [KROWS, H, T], bf16)
        negmax = sb("negmax", [P, 2, 16])
        nm_rows = sb("nm_rows", [16, 2, 2, P], bf16)
        v_stage = sb("v_stage", [P, TB, C])
        V = sb("V", [P, TB, H, VW])
        probs = sb("probs", [P, RING, T])
        o_raw = sb("o_raw", [P, T])
        rsum = sb("rsum", [P, 2, TB, 4])
        o_n = sb("o_n", [P, TB, C])
        oT = sb("oT", [P, T])
        mix_a = sb("mix_a", [P, T])
        mix_b = sb("mix_b", [P, T])
        xrT = sb("xrT", [P, T])
        xkT = sb("xkT", [P, T])
        th = sb("th", [P, TB, C])
        gate = sb("gate", [P, TB, C])
        relu = sb("relu", [P, T])
        kact = sb("kact", [P, T])
        kv_sb = sb("kv_sb", [P, TB, C])
        ffn = sb("ffn", [P, TB, C])
        xb = sb("xb", [P, TB, C])
        res_next = sb("res_next", [P, TB, C])
        res = sb("res", [P, TB, C])
        y_sb = sb("y_sb", [P, TB, C])

        max_ps = ctx.enter_context(nc.psum_tensor("max_ps", [P, 3, T], fp32))
        sc_ps = ctx.enter_context(nc.psum_tensor("sc_ps", [P, 3, T], fp32))
        av_ps = ctx.enter_context(nc.psum_tensor("av_ps", [P, T], fp32))
        sh_ps = ctx.enter_context(nc.psum_tensor("sh_ps", [P, T], fp32))
        sh_tok = sh_ps[:, :].rearrange("p (j c) -> p j c", j=TB)
        sh_heads = sh_ps[:, :].rearrange("p (j h w) -> p j h w", j=TB, w=VW)
        sh_m = sh_ps[0:16, 0:P]

        def product_of(n, b):
            return sc_ps[:, 0, :] if n == 1 and isinstance(b, int) and b == 0 else sh_ps[:, :]

        x_first_loaded = sem("x_first_loaded")
        x_early_loaded = sem("x_early_loaded")
        x_late_loaded = sem("x_late_loaded")
        cols_loaded = sem("cols_loaded")
        weights_loaded = sem("weights_loaded")
        tables_loaded = sem("tables_loaded")
        rows_loaded = sem("rows_loaded")
        ident_loaded = sem("ident_loaded")
        krel_loaded = sem("krel_loaded")
        first_loaded = sem("first_loaded")
        qrel_loaded = sem("qrel_loaded")
        scratch_written = [sem(f"scratch_{n}_written") for n in "qk"]
        slab_loaded = [sem(f"slab{g}_loaded") for g in range(G)]
        m_loaded = [sem(f"m{g}_loaded") for g in range(G)]
        y_stored = sem("y_stored")
        max_tile = sem("max_tile")
        score_tile = sem("score_tile")
        av_step = sem("av_step")
        xnT_made = sem("xnT_made")
        xaT_made = sem("xaT_made")
        q_made = sem("q_made")
        k_made = sem("k_made")
        v_made = sem("v_made")
        r_made = sem("r_made")
        kf_made = sem("kf_made")
        kv_made = sem("kv_made")
        m_made = sem("m_made")
        o_made = sem("o_made")
        onT_made = sem("onT_made")
        out_made = sem("out_made")
        rows_maxed = sem("rows_maxed")
        probs_ready = sem("probs_ready")
        small_ready = sem("small_ready")
        zeros_ready = sem("zeros_ready")
        stats_ready = sem("stats_ready")
        ln_chain = sem("ln_chain")
        later_stats = sem("later_stats")
        less_mean = sem("less_mean")
        xn_ready = sem("xn_ready")
        xa_ready = sem("xa_ready")
        xnT_ready = sem("xnT_ready")
        xaT_ready = sem("xaT_ready")
        high_ready = [sem(f"high_{n}_ready") for n in "qk"]
        left_ready = [sem(f"left_{n}_ready") for n in "qk"]
        mid_ready = [sem(f"mid_{n}_ready") for n in "qk"]
        parts_ready = [sem(f"parts_{n}_ready") for n in "qk"]
        rel_terms_ready = sem("rel_terms_ready")
        rel_left_ready = sem("rel_left_ready")
        rel_summed = sem("rel_summed")
        rel_parts_ready = sem("rel_parts_ready")
        m_high = sem("m_high")
        m_low = sem("m_low")
        v_staged = sem("v_staged")
        v_ready = sem("v_ready")
        mix_chain = sem("mix_chain")
        xr_ready = sem("xr_ready")
        xk_ready = sem("xk_ready")
        th_ready = sem("th_ready")
        relu_ready = sem("relu_ready")
        gate_ready = sem("gate_ready")
        kact_ready = sem("kact_ready")
        xb_ready = sem("xb_ready")
        kv_read = sem("kv_read")
        ffn_ready = sem("ffn_ready")
        res_next_ready = sem("res_next_ready")
        res_ready = sem("res_ready")
        o_raw_ready = sem("o_raw_ready")
        rsum_ready = sem("rsum_ready")
        o_n_ready = sem("o_n_ready")
        oT_ready = sem("oT_ready")
        y_ready = sem("y_ready")
        waited = sem("waited")

        block = ctx.enter_context(nc.Block())

        def bodies(eng, body):
            body("first", 0)
            with eng.Fori(1, B - 1) as b:
                body("middle", b)
            body("last", B - 1)

        def chain(eng, sem_, base):
            done = [base]

            def link(ins):
                ins.then_inc(sem_, 1)
                done[0] = done[0] + 1
                eng.wait_ge(sem_, done[0])
            return link

        def positive(v):
            return not isinstance(v, int) or v > 0

        def settle(eng):
            eng.sem_inc(waited, 1)

        @block.sync
        def _(sp):
            def write_scratch(n):
                sp.dma_start(scratch[n].rearrange("a p t -> p a t"), parts[n][:, :, :]).then_inc(scratch_written[n], 16)

            by_dim = scratch.rearrange("n a (d h) t -> n a d h t", h=H)

            def load_q(g):
                hs = slice(4 * g, 4 * g + 4)
                for row, n in ((0, 3), (3, 2), (5, 1)):
                    sp.dma_start(Q[row * HD:(row + n) * HD, hs, :],
                                 by_dim[0, 0:n, :, hs, :].rearrange("a d h t -> (a d) h t")).then_inc(slab_loaded[g], 16)

            def load_k(g):
                hs = slice(4 * g, 4 * g + 4)
                for part, (row, n) in enumerate(((0, 3), (3, 2), (5, 1))):
                    sp.dma_start(K[row * HD:(row + n) * HD, hs, :],
                                 by_dim[1, part:part + 1, :, hs, :].to_broadcast([n, HD, 4, T])).then_inc(slab_loaded[g], 16)

            def load_m(g, b):
                after = (b - 1) * 4 * STEPS + 16 * (g + 1)
                if positive(after):
                    sp.wait_ge(score_tile, after)
                    settle(sp)
                for p, ready in enumerate((m_high, m_low)):
                    sp.wait_ge(ready, 4 * b + g + 1)
                    settle(sp)
                    sp.dma_start(Q[KMAX + p:KMAX + p + 1, 4 * g:4 * g + 4, :],
                                 nm_rows[:, g % 2, p, :]).then_inc(m_loaded[g], 16)

            def slab(g, b):
                after = (b - 1) * 4 * STEPS + 16 * (g + 1)
                if positive(after):
                    sp.wait_ge(score_tile, after)
                    settle(sp)
                load_q(g)
                load_k(g)

            def store(b):
                sp.wait_ge(y_ready, b + 1)
                settle(sp)
                sp.dma_start(out[bass.ds(b, 1)].rearrange("o (j p) c -> p (o j) c", p=P), y_sb[:, :, :]).then_inc(y_stored, 16)

            sp.dma_start(x_all[:, 0], x[0].rearrange("(j p) c -> p j c", p=P)).then_inc(x_first_loaded, 16)
            sp.dma_start(c_sb[:, :], cols).then_inc(cols_loaded, 16)
            sp.dma_start(tab[:, :, :], rel_tab).then_inc(tables_loaded, 16)
            sp.dma_start(idf[:, :], ident).then_inc(ident_loaded, 16)
            sp.dma_start(w_sb[:, :, :], weights).then_inc(weights_loaded, 16)
            sp.dma_start(x_all[:, 1:EARLY], x[1:EARLY].rearrange("b (j p) c -> p b j c", p=P)).then_inc(x_early_loaded, 16)
            sp.dma_start(K[KREL:KROWS, :, :], k_rel[:, None, :].to_broadcast([KROWS - KREL, H, T])).then_inc(krel_loaded, 16)
            sp.dma_start(x_all[:, EARLY:], x[EARLY:].rearrange("b (j p) c -> p b j c", p=P)).then_inc(x_late_loaded, 16)
            sp.dma_start(row_sb[:, :, :], rows.partition_broadcast(P)).then_inc(rows_loaded, 16)

            def direct(operand, of, part, first, src, signal):
                for row, p in enumerate(of):
                    if p == part:
                        sp.dma_start(operand[first + row * HD:first + (row + 1) * HD, :, :],
                                     src[:, part, :]).then_inc(signal, 16)

            for part in range(3):
                sp.wait_ge(rel_parts_ready, part + 1)
                direct(Q, Q_PARTS, part, KREL, rel_parts, qrel_loaded)
            for part, done in enumerate((high_ready, mid_ready, parts_ready)):
                for n in range(2):
                    sp.wait_ge(done[n], 1)
                    direct((Q, K)[n], (Q_PARTS, K_PARTS)[n], part, 0, parts[n], first_loaded)
            load_m(0, 0)

            def body(kind, b):
                load_m(1, b)
                if kind == "last":
                    store(b - 1)
                    load_m(2, b)
                    load_m(3, b)
                    return
                if positive(b):
                    for g in range(G):
                        sp.wait_ge(slab_loaded[g], 6 * 16 * b)
                        settle(sp)
                for n in range(2):
                    sp.wait_ge(parts_ready[n], b + 2)
                    settle(sp)
                    write_scratch(n)
                if kind != "first":
                    store(b - 1)
                for n in range(2):
                    sp.wait_ge(scratch_written[n], 16 * (b + 1))
                    settle(sp)
                slab(0, b + 1)
                load_m(2, b)
                slab(1, b + 1)
                load_m(3, b)
                slab(2, b + 1)
                load_m(0, b + 1)
                slab(3, b + 1)

            bodies(sp, body)
            store(B - 1)
            sp.wait_ge(y_stored, 16 * B)

        @block.tensor
        def _(pe):
            last_use = []

            def take_bank(name, b):
                if last_use:
                    before, of = last_use
                    count = of + 1
                    if before[0] == "m":
                        done, count = m_low, 4 * of + int(before[1]) + 1
                    elif before[0] == "o" and before[1].isdigit():
                        done, count = o_n_ready, 4 * of + int(before[1]) + 1
                    else:
                        done = {"xnT": xnT_ready, "xaT": xaT_ready, "q": left_ready[0], "k": left_ready[1],
                                "v": v_staged, "r": th_ready, "kf": relu_ready, "kv": kv_read,
                                "onT": oT_ready, "out": y_ready}[before]
                    pe.wait_ge(done, count)
                last_use[:] = name, b

            def transposes(src, made, ready=None, base=0):
                for j in range(TB):
                    if ready is not None:
                        pe.wait_ge(ready, base + j + 1)
                    last = nc.tensor.transpose(sh_ps[:, j * P:(j + 1) * P], src[:, j * P:(j + 1) * P], idf[:, :])
                last.then_inc(made, 1)

            def by_token(lhs, w, made):
                for j in range(TB):
                    last = nc.tensor.matmul(sh_ps[:, j * P:(j + 1) * P], lhs[:, j * P:(j + 1) * P],
                                            w_sb[:, w, :], start=True, stop=True)
                last.then_inc(made, 1)

            def by_channel(w, rhs, made):
                nc.tensor.matmul(sh_ps[:, :], w_sb[:, w, :], rhs[:, :], start=True, stop=True).then_inc(made, 1)

            flat = "p j c -> p (j c)"

            def use(name, b):
                take_bank(name, b)
                if name == "xnT":
                    transposes(xn_tok[:, :, :].rearrange(flat), xnT_made, xn_ready, 4 * b)
                elif name == "xaT":
                    transposes(xa_tok[:, :, :].rearrange(flat), xaT_made, xa_ready, 4 * b)
                elif name == "q":
                    pe.wait_ge(xaT_ready, b + 1)
                    by_channel(W_Q, xaT, q_made)
                elif name == "k":
                    by_channel(W_K, xaT, k_made)
                elif name == "v":
                    by_token(xaT, W_V, v_made)
                elif name == "r":
                    pe.wait_ge(xr_ready, b + 1)
                    by_token(xrT, W_R, r_made)
                elif name == "kf":
                    pe.wait_ge(xk_ready, b + 1)
                    by_channel(W_KF, xkT, kf_made)
                elif name == "kv":
                    pe.wait_ge(kact_ready, b + 1)
                    by_token(kact, W_VF, kv_made)
                elif name[0] == "m":
                    g = int(name[1])
                    pe.wait_ge(rows_maxed, b * 4 * STEPS + 16 * (g + 1))
                    nc.tensor.transpose(sh_m, negmax[:, g % 2, :], idf[:, :]).then_inc(m_made, 1)
                elif name == "onT":
                    pe.wait_ge(o_n_ready, 4 * (b + 1))
                    transposes(o_n[:, :, :].rearrange(flat), onT_made)
                elif name == "out":
                    pe.wait_ge(oT_ready, b + 1)
                    by_token(oT, W_O, out_made)
                else:
                    pe.wait_ge(o_raw_ready, 4 * b + int(name[1]) + 1)
                    transposes(o_raw, o_made)

            def max_tile_of(tile, b):
                head, i = tile // TB, tile % TB
                pos, g = head, head // 4
                n = b * 4 * STEPS + tile
                if pos % 4 == 0 and i == 0 and positive(b):
                    pe.wait_ge(slab_loaded[g], 6 * 16 * b)
                free = n - since_bank(4 * pos + i) + 1
                if positive(free):
                    pe.wait_ge(rows_maxed, free)
                nc.tensor.matmul(max_ps[:, bank(4 * pos + i), :], Q[0:KMAX, head, i * P:(i + 1) * P], K[0:KMAX, head, :],
                                 start=True, stop=True).then_inc(max_tile, 1)

            def score_tile_of(s, b, i):
                g, kt = s // 4, s % 4
                n = b * 4 * STEPS + 4 * s + i
                if kt == 0 and i == 0:
                    pe.wait_ge(m_loaded[g], 32 * (b + 1))
                free = n - since_bank(4 * s + i) + 1
                if positive(free):
                    pe.wait_ge(probs_ready, free)
                head = 4 * g + i
                nc.tensor.matmul(sc_ps[:, bank(4 * s + i), :], K[:, head, kt * P:(kt + 1) * P], Q[:, head, :],
                                 start=True, stop=True).then_inc(score_tile, 1)

            def av(s, b):
                g, kt = s // 4, s % 4
                pe.wait_ge(probs_ready, b * 4 * STEPS + 4 * s + 4)
                if kt == 0:
                    pe.wait_ge(v_ready, 4 * b + g + 1)
                    if positive(4 * b + g):
                        pe.wait_ge(o_raw_ready, 4 * b + g)
                for i in range(4):
                    last = nc.tensor.matmul(av_ps[VW * i:VW * (i + 1), :], V[:, kt, 4 * g + i, :],
                                            probs[:, (4 * s + i) % RING, :], start=kt == 0, stop=kt == TB - 1)
                last.then_inc(av_step, 1)

            pe.wait_ge(ident_loaded, 16)
            for _ in range(WARM_UP):
                nc.tensor.transpose(av_ps[:, 0:P], idf[:, :], idf[:, :])
            use("xaT", 0)
            pe.wait_ge(weights_loaded, 16)
            use("q", 0)
            nc.tensor.matmul(sc_ps[:, 0, :], w_sb[:, W_K, :], xaT[:, :], start=True, stop=True).then_inc(k_made, 1)
            for name in ("xnT", "v", "r", "kf"):
                use(name, 0)
            pe.wait_ge(krel_loaded, 16)
            pe.wait_ge(qrel_loaded, 16 * NPROD)
            pe.wait_ge(first_loaded, 2 * 16 * NPROD)
            pe.wait_ge(left_ready[1], 1)
            for t in range(4 * LEAD):
                max_tile_of(t, 0)
                if t == 16:
                    use("m0", 0)
                elif t == 18:
                    use("kv", 0)

            def body(kind, b):
                of = {"prev": b - 1, "this": b, "next": b + 1}
                last_use[:] = ("kv" if kind == "first" else "m0"), b
                for s in range(STEPS):
                    for i in range(4):
                        ahead = 4 * (s + LEAD) + i
                        if ahead < 4 * STEPS:
                            max_tile_of(ahead, b)
                        elif kind != "last":
                            max_tile_of(ahead - 4 * STEPS, b + 1)
                        score_tile_of(s, b, i)
                        if i == AV_AFTER[kind] and s > 0:
                            av(s - 1, b)
                        elif i == AV_AFTER[kind] and kind != "first":
                            av(STEPS - 1, b - 1)
                        if i < 3 and plan(kind, s, i) is not None:
                            name, whose = plan(kind, s, i)
                            use(name, of[whose])

            bodies(pe, body)
            av(STEPS - 1, B - 1)
            for name in ("o3", "onT", "out"):
                use(name, B - 1)

        @block.scalar
        def _(act):
            def exp_tile(s, b, i):
                n = b * 4 * STEPS + 4 * s + i
                if i == 0:
                    before = b * STEPS + s - RING // 4 + 1
                    if positive(before):
                        act.wait_ge(av_step, before)
                act.wait_ge(score_tile, n + 1)
                nc.scalar.activation(probs[:, (4 * s + i) % RING, :], sc_ps[:, bank(4 * s + i), :], ACT.Exp,
                                     scale=SCALE).then_inc(probs_ready, 1)

            def read_av(s, b):
                act.wait_ge(av_step, b * STEPS + s + 1)
                n = 4 * b + s // 4
                if positive(n):
                    act.wait_ge(o_made, n)
                nc.scalar.copy(o_raw[:, :], av_ps[:, :]).then_inc(o_raw_ready, 1)

            def read_out(name, b):
                if name == "xnT":
                    act.wait_ge(xnT_made, b + 1)
                    if positive(b):
                        act.wait_ge(xk_ready, b)
                    ins, done = nc.scalar.copy(xnT[:, 1:], sh_ps[:, :]), xnT_ready
                elif name == "xaT":
                    act.wait_ge(xaT_made, b + 1)
                    if positive(b):
                        act.wait_ge(v_made, b)
                    ins, done = nc.scalar.activation(xaT[:, :], sh_ps[:, :], ACT.Identity, bias=c_sb[:, C_B:C_B + 1],
                                                     scale=c_sb[:, C_G:C_G + 1]), xaT_ready
                elif name in ("q", "k"):
                    n = "qk".index(name)
                    act.wait_ge((q_made, k_made)[n], b + 1)
                    if isinstance(b, int) and b == 1:
                        act.wait_ge(first_loaded, 2 * 16 * NPROD)
                    elif positive(b):
                        act.wait_ge(scratch_written[n], 16 * (b - 1))
                    bias = (C_BQ, C_BK)[n]
                    ins, done = nc.scalar.activation(parts[n][:, 0, :], product_of(n, b), ACT.Identity,
                                                     bias=c_sb[:, bias:bias + 1]), high_ready[n]
                elif name == "r":
                    act.wait_ge(r_made, b + 1)
                    if positive(b):
                        act.wait_ge(gate_ready, b)
                    ins, done = nc.scalar.activation(th[:, :, :], sh_tok, ACT.Tanh, scale=0.5), th_ready
                elif name == "kf":
                    act.wait_ge(kf_made, b + 1)
                    if positive(b):
                        act.wait_ge(kact_ready, b)
                    ins, done = nc.scalar.activation(relu[:, :], sh_ps[:, :], ACT.Relu), relu_ready
                elif name == "v":
                    act.wait_ge(v_made, b + 1)
                    if positive(4 * b):
                        act.wait_ge(v_ready, 4 * b)
                    ins, done = nc.scalar.copy(v_stage[:, :, :], sh_tok), v_staged
                elif name == "kv":
                    act.wait_ge(kv_made, b + 1)
                    if positive(b):
                        act.wait_ge(ffn_ready, b)
                    ins, done = nc.scalar.copy(kv_sb[:, :, :], sh_tok), kv_read
                elif name == "onT":
                    act.wait_ge(onT_made, b + 1)
                    if positive(b):
                        act.wait_ge(out_made, b)
                    ins, done = nc.scalar.copy(oT[:, :], sh_ps[:, :]), oT_ready
                elif name[0] == "m":
                    g = int(name[1])
                    act.wait_ge(m_made, 4 * b + g + 1)
                    before = b if g >= 2 else b - 1
                    if positive(before + (g >= 2)):
                        act.wait_ge(m_loaded[(g + 2) % 4], 32 * (before + 1))
                    ins, done = nc.scalar.copy(nm_rows[:, g % 2, 0, :], sh_m), m_high
                else:
                    return
                ins.then_inc(done, 1)

            act.wait_ge(cols_loaded, 16)
            nc.scalar.activation(table_in[:, :], c_sb[:, 0:1], ACT.Exp)
            for name in ("xaT", "q", "k", "xnT", "v", "r", "kf", "m0", "kv"):
                read_out(name, 0)

            def body(kind, b):
                of = {"prev": b - 1, "this": b, "next": b + 1}
                for s in range(STEPS):
                    for i in range(4):
                        exp_tile(s, b, i)
                        if i == AV_AFTER[kind] and s % 4 == 0 and s > 0:
                            read_av(s - 1, b)
                        elif i == AV_AFTER[kind] and s == 0 and kind != "first":
                            read_av(STEPS - 1, b - 1)
                        if i < 3 and plan(kind, s, i) is not None:
                            name, whose = plan(kind, s, i)
                            read_out(name, of[whose])

            bodies(act, body)
            read_av(STEPS - 1, B - 1)
            read_out("onT", B - 1)

        @block.vector
        def _(dve):
            ln = chain(dve, ln_chain, 0)

            def raw_statistics(bs):
                for b in bs:
                    for j in range(TB):
                        nc.vector.bn_stats(stats[:, b, j, :], x_all[:, b, j, :]).then_inc(stats_ready, 1)

            def scales(bs):
                return (a[:, :, bs[0] * TB:(bs[-1] + 1) * TB] for a in (lnw, lny, lnt))

            def statistics(bs):
                n0, n1 = bs[0] * TB, (bs[-1] + 1) * TB
                dve.wait_ge(stats_ready, n1)
                for n in range(n0, n1):
                    last = nc.vector.bn_aggr(moments[:, n, :], stats[:, n // TB, n % TB, :])
                ln(last)
                var = moments[:, n0:n1, 1]
                w, y, _ = scales(bs)
                nc.vector.tensor_scalar(lnw[:, 0, n0:n1], var, EPS, None, ALU.add)
                ln(nc.vector.tensor_scalar(lnw[:, 1, n0:n1], var, 1.0 + EPS, EPS * EPS, ALU.mult, ALU.add))
                ln(nc.vector.tensor_scalar(y.bitcast(i32), w.bitcast(i32), -0.5, float(0x5f3759df), ALU.mult, ALU.add))

            def newton(bs, steps):
                w, y, t = scales(bs)
                for _ in range(steps):
                    ln(nc.vector.scalar_tensor_tensor(t, y, -0.5, y, ALU.mult, ALU.mult))
                    ln(nc.vector.tensor_tensor(t, t, w, ALU.mult))
                    ln(nc.vector.scalar_tensor_tensor(y, t, 1.5, y, ALU.add, ALU.mult))

            def normalise(which):
                for j in range(TB):
                    nc.vector.tensor_scalar((xn_tok, xa_tok)[which][:, j, :], x_all[:, 0, j, :], moments[:, j, 0:1],
                                            lny[:, which, j:j + 1],
                                            ALU.subtract, ALU.mult).then_inc((xn_ready, xa_ready)[which], 1)

            def reduce_tile(tile, b):
                n = b * 4 * STEPS + tile
                pos, i = tile // 4, tile % 4
                g = pos // 4
                if pos % 4 == 0 and i == 0:
                    before = 4 * b + g - 1
                    if positive(before):
                        dve.wait_ge(m_made, before)
                dve.wait_ge(max_tile, n + 1)
                col = 4 * (pos % 4) + i
                nc.vector.tensor_reduce(negmax[:, g % 2, col:col + 1], max_ps[:, bank(4 * pos + i), :], AX.X, ALU.max,
                                        negate=True).then_inc(rows_maxed, 1)

            def read_out(name, b):
                if name in ("q", "k"):
                    n = "qk".index(name)
                    dve.wait_ge(high_ready[n], b + 1)
                    if positive(b):
                        dve.wait_ge(parts_ready[n], b)
                    bias = (C_BQ, C_BK)[n]
                    ins = nc.vector.scalar_tensor_tensor(left[n][:, :], product_of(n, b), c_sb[:, bias:bias + 1],
                                                         parts[n][:, 0, :], ALU.add, ALU.subtract)
                    ins.then_inc(left_ready[n], 1)
                elif name == "out":
                    dve.wait_ge(out_made, b + 1)
                    dve.wait_ge(res_ready, b + 1)
                    if positive(b):
                        dve.wait_ge(y_stored, 16 * b)
                    ins = nc.vector.tensor_tensor(y_sb[:, :, :], sh_tok, res[:, :, :], ALU.add)
                    ins.then_inc(y_ready, 1)
                elif name[0] == "m":
                    g = int(name[1])
                    dve.wait_ge(m_high, 4 * b + g + 1)
                    before = b if g >= 2 else b - 1
                    if positive(before + (g >= 2)):
                        dve.wait_ge(m_loaded[(g + 2) % 4], 32 * (before + 1))
                    nc.vector.tensor_tensor(nm_rows[:, g % 2, 1, :], sh_m, nm_rows[:, g % 2, 0, :],
                                            ALU.subtract).then_inc(m_low, 1)
                    return
                elif name[0] == "o" and name != "onT":
                    g = int(name[1])
                    dve.wait_ge(o_made, 4 * b + g + 1)
                    nc.vector.reciprocal(rsum[:, g % 2], sh_heads[:, :, :, HD]).then_inc(rsum_ready, 1)
                    if g == 0 and positive(b):
                        dve.wait_ge(onT_made, b)
                    dve.wait_ge(rsum_ready, 4 * b + g + 1)
                    heads = o_n[:, :, :].rearrange("p j (h d) -> p j h d", d=HD)[:, :, 4 * g:4 * g + 4, :]
                    ins = nc.vector.tensor_tensor(heads, sh_heads[:, :, :, 0:HD],
                                                  rsum[:, g % 2][:, :, :, None].to_broadcast([P, TB, 4, HD]), ALU.mult)
                    ins.then_inc(o_n_ready, 1)

            dve.wait_ge(x_first_loaded, 16)
            raw_statistics([0])
            statistics([0])
            newton([0], 3)
            dve.wait_ge(cols_loaded, 16)
            normalise(1)
            normalise(0)
            dve.wait_ge(x_early_loaded, 16)
            raw_statistics(range(1, EARLY))
            read_out("q", 0)
            read_out("k", 0)
            dve.wait_ge(left_ready[1], 1)
            nc.vector.tensor_copy(parts[1][:, 1, :], left[1][:, :]).then_inc(mid_ready[1], 1)
            dve.wait_ge(mid_ready[1], 1)
            nc.vector.tensor_tensor(parts[1][:, 2, :], left[1][:, :], parts[1][:, 1, :],
                                    ALU.subtract).then_inc(parts_ready[1], 1)
            dve.wait_ge(x_late_loaded, 16)
            raw_statistics(range(EARLY, B))
            statistics(range(1, B))
            dve.sem_inc(later_stats, 1)
            newton(range(1, B), 2)
            for t in range(4 * LEAD):
                reduce_tile(t, 0)
                if t == 16:
                    read_out("m0", 0)
                    newton(range(1, B), 1)
                    dve.sem_inc(later_stats, 1)

            def body(kind, b):
                of = {"prev": b - 1, "this": b, "next": b + 1}
                held = None
                for s in range(STEPS):
                    for i in range(4):
                        ahead = 4 * (s + LEAD) + i
                        if ahead < 4 * STEPS:
                            reduce_tile(ahead, b)
                        elif kind != "last":
                            reduce_tile(ahead - 4 * STEPS, b + 1)
                        if held is not None:
                            read_out(*held)
                            held = None
                        if i < 3 and plan(kind, s, i) is not None:
                            name, whose = plan(kind, s, i)
                            if name in ("q", "k", "m0", "m1", "m2", "m3"):
                                held = name, of[whose]
                            else:
                                read_out(name, of[whose])

            bodies(dve, body)
            read_out("o3", B - 1)
            read_out("out", B - 1)

        @block.gpsimd
        def _(pool):
            def cast(dst, src):
                settle(pool)
                return nc.gpsimd.tensor_scalar(dst, src, 1.0, 0.0, ALU.mult, ALU.add)

            def normalise(b):
                def by_token(a):
                    return a[:, :, None].to_broadcast([P, TB, C])

                tokens = bass.ds(b * TB, TB)
                if isinstance(b, int):
                    pool.wait_ge(later_stats, 1)
                    settle(pool)
                nc.gpsimd.tensor_tensor(x_less_mean[:, :, :], x_all[:, bass.ds(b, 1)].rearrange("p o j c -> p (o j) c"),
                                        by_token(moments[:, tokens, 0]), ALU.subtract).then_inc(less_mean, 1)
                for which, dst, made, ready in ((1, xa_tok, xaT_made, xa_ready), (0, xn_tok, xnT_made, xn_ready)):
                    if isinstance(b, int):
                        pool.wait_ge(later_stats, 2)
                    pool.wait_ge(less_mean, b)
                    pool.wait_ge(made, b)
                    settle(pool)
                    nc.gpsimd.tensor_tensor(dst[:, :, :], x_less_mean[:, :, :], by_token(lny[:, which, tokens]),
                                            ALU.mult).then_inc(ready, 4)

            def split(n, b):
                pool.wait_ge(left_ready[n], b + 1)
                r, p = left[n], parts[n]
                cast(p[:, 1, :], r[:, :]).then_inc(mid_ready[n], 1)
                pool.wait_ge(mid_ready[n], b + 1)
                nc.gpsimd.tensor_tensor(p[:, 2, :], r[:, :], p[:, 1, :], ALU.subtract).then_inc(parts_ready[n], 1)

            def place_v(g, b):
                pool.wait_ge(v_staged, b + 1)
                after = (b - 1) * STEPS + 4 * (g + 1)
                if positive(after):
                    pool.wait_ge(av_step, after)
                cols_of = slice(4 * HD * g, 4 * HD * (g + 1))
                for j in range(TB):
                    last = nc.gpsimd.tensor_tensor(V[:, j, 4 * g:4 * g + 4, 0:HD],
                                                   v_stage[:, j, cols_of].rearrange("p (h d) -> p h d", d=HD),
                                                   row_sb[:, 0, cols_of].rearrange("p (h d) -> p h d", d=HD), ALU.add)
                last.then_inc(v_ready, 1)

            def mix(b):
                pool.wait_ge(xnT_ready, b + 1)
                link = chain(pool, mix_chain, 2 * b)
                for n, (mu, dst, made, ready) in enumerate(((C_MUR, xrT, r_made, xr_ready), (C_MUK, xkT, kf_made, xk_ready))):
                    if n == 1:
                        pool.wait_ge(xr_ready, b + 1)
                    elif positive(b):
                        pool.wait_ge(xk_ready, b)
                    settle(pool)
                    nc.gpsimd.tensor_scalar(mix_a[:, :], xnT[:, 1:], c_sb[:, mu:mu + 1], 0.0, ALU.mult, ALU.add)
                    link(nc.gpsimd.tensor_scalar(mix_b[:, :], xnT[:, 0:T], mu_rest[:, n:n + 1], 0.0, ALU.mult, ALU.add))
                    if positive(b):
                        pool.wait_ge(made, b)
                    nc.gpsimd.tensor_tensor(dst[:, :], mix_a[:, :], mix_b[:, :], ALU.add).then_inc(ready, 1)

            def x_and_bias(b):
                if positive(b):
                    pool.wait_ge(res_next_ready, b)
                    settle(pool)
                nc.gpsimd.tensor_tensor(xb[:, :, :], x_all[:, bass.ds(b, 1)].rearrange("p o j c -> p (o j) c"),
                                        row_sb[:, 1:2, :].to_broadcast([P, TB, C]), ALU.add).then_inc(xb_ready, 1)

            def gate_of(b):
                pool.wait_ge(th_ready, b + 1)
                if positive(b):
                    pool.wait_ge(ffn_ready, b)
                settle(pool)
                nc.gpsimd.tensor_scalar(gate[:, :, :], th[:, :, :], 0.5, 0.5, ALU.mult, ALU.add).then_inc(gate_ready, 1)

            def square(b):
                pool.wait_ge(relu_ready, b + 1)
                if positive(b):
                    pool.wait_ge(kv_made, b)
                nc.gpsimd.tensor_tensor(kact[:, :], relu[:, :], relu[:, :], ALU.mult).then_inc(kact_ready, 1)

            def gated(b):
                pool.wait_ge(kv_read, b + 1)
                pool.wait_ge(gate_ready, b + 1)
                if positive(b):
                    pool.wait_ge(res_next_ready, b)
                nc.gpsimd.tensor_tensor(ffn[:, :, :], kv_sb[:, :, :], gate[:, :, :], ALU.mult).then_inc(ffn_ready, 1)

            def residual(b):
                pool.wait_ge(ffn_ready, b + 1)
                pool.wait_ge(xb_ready, b + 1)
                if positive(b):
                    pool.wait_ge(res_ready, b)
                nc.gpsimd.tensor_tensor(res_next[:, :, :], ffn[:, :, :], xb[:, :, :], ALU.add).then_inc(res_next_ready, 1)

            def hand_over(b):
                pool.wait_ge(res_next_ready, b + 1)
                if positive(b):
                    pool.wait_ge(y_ready, b)
                settle(pool)
                cast(res[:, :, :], res_next[:, :, :]).then_inc(res_ready, 1)

            nc.gpsimd.memset(xnT[:, 0:1], 0.0).then_inc(zeros_ready, 1)
            nc.gpsimd.memset(V[:, :, :, HD:VW], 0.0).then_inc(zeros_ready, 1)
            pool.wait_ge(zeros_ready, 2)
            nc.gpsimd.memset(V[:, :, :, HD:HD + 1], 1.0).then_inc(zeros_ready, 1)
            pool.wait_ge(zeros_ready, 3)
            pool.wait_ge(cols_loaded, 16)
            nc.gpsimd.tensor_scalar(rel_w[:, :], c_sb[:, C_WS:C_WC + 1], 1.0 / SCALE, 0.0, ALU.mult, ALU.add).then_inc(small_ready, 1)
            for n, c in enumerate((C_MUR, C_MUK)):
                nc.gpsimd.tensor_scalar(mu_rest[:, n:n + 1], c_sb[:, c:c + 1], -1.0, 1.0, ALU.mult,
                                        ALU.add).then_inc(small_ready, 1)
            pool.wait_ge(small_ready, 3)
            pool.wait_ge(tables_loaded, 16)
            nc.gpsimd.tensor_scalar(rel_full[:, :], tab[:, 0, :], rel_w[:, 0:1], 0.0, ALU.mult, ALU.add)
            nc.gpsimd.tensor_scalar(rel_left[:, :], tab[:, 1, :], rel_w[:, 1:2], 0.0, ALU.mult, ALU.add).then_inc(rel_terms_ready, 1)
            pool.wait_ge(rel_terms_ready, 1)
            nc.gpsimd.tensor_tensor(rel_full[:, :], rel_full[:, :], rel_left[:, :], ALU.add).then_inc(rel_summed, 1)
            pool.wait_ge(rel_summed, 1)
            part_done = chain(pool, rel_parts_ready, 0)
            part_done(cast(rel_parts[:, 0, :], rel_full[:, :]))
            nc.gpsimd.tensor_tensor(rel_left[:, :], rel_full[:, :], rel_parts[:, 0, :], ALU.subtract).then_inc(rel_left_ready, 1)
            pool.wait_ge(rel_left_ready, 1)
            part_done(cast(rel_parts[:, 1, :], rel_left[:, :]))
            nc.gpsimd.tensor_tensor(rel_parts[:, 2, :], rel_left[:, :], rel_parts[:, 1, :],
                                    ALU.subtract).then_inc(rel_parts_ready, 1)
            split(0, 0)
            mix(0)
            pool.wait_ge(rows_loaded, 16)
            place_v(0, 0)
            gate_of(0)
            square(0)
            for g in range(1, G):
                place_v(g, 0)
            x_and_bias(0)
            normalise(1)
            gated(0)
            residual(0)

            def body(kind, b):
                if kind == "middle":
                    normalise(b + 1)
                if kind != "first":
                    place_v(3, b)
                if kind != "last":
                    mix(b + 1)
                    split(0, b + 1)
                    split(1, b + 1)
                hand_over(b)
                if kind != "last":
                    place_v(0, b + 1)
                    gate_of(b + 1)
                    square(b + 1)
                    x_and_bias(b + 1)
                    gated(b + 1)
                    residual(b + 1)
                    place_v(1, b + 1)
                    place_v(2, b + 1)

            bodies(pool, body)


def kernel(L0_attn_x, L0_attn_ln_g, L0_attn_ln_b, L0_attn_w_qkv, L0_attn_b_qkv, L0_attn_w_rel, L0_attn_w_out,
           L0_attn_b_out, L0_ffn_W_r, L0_ffn_W_k, L0_ffn_W_v, L0_ffn_mu_r, L0_ffn_mu_k):
    import ml_dtypes

    import concourse.bacc as bacc
    from concourse.bass_utils import run_bass_kernel_spmd

    bf = ml_dtypes.bfloat16
    a = np.asarray
    w = a(L0_attn_w_qkv).reshape(C, 3, H, HD)
    bias = a(L0_attn_b_qkv).reshape(3, H, HD)
    dim_major = lambda m: np.swapaxes(m, -1, -2).reshape(*m.shape[:-2], C)
    weights = np.stack([dim_major(w[:, 0]), dim_major(w[:, 1]), w[:, 2].reshape(C, C), a(L0_ffn_W_r).T,
                        a(L0_ffn_W_k).T, a(L0_ffn_W_v).T, a(L0_attn_w_out)], axis=1)
    rel = np.repeat(a(L0_attn_w_rel).reshape(HD // 2, 2, H), 2, axis=0)
    cols = np.stack([a(L0_attn_ln_g), a(L0_attn_ln_b), dim_major(bias[0]), dim_major(bias[1]), a(L0_ffn_mu_r),
                     a(L0_ffn_mu_k), rel[:, 0].reshape(C), rel[:, 1].reshape(C)], axis=1)
    rows = np.stack([bias[2].reshape(C), a(L0_attn_b_out)])

    div = np.exp(np.arange(0, HD, 2, dtype=np.float32) * np.float32(-np.log(10000.0) / HD)).astype(np.float64)
    angle = div[:, None] * np.arange(T)
    sin, cos = np.sin(angle), np.cos(angle)
    table = np.stack([np.stack([sin, -cos], 1), np.stack([cos, sin], 1)])
    rel_tab = np.repeat(table.reshape(2, HD, 1, T), H, axis=2).reshape(2, C, T).transpose(1, 0, 2).astype(np.float32)
    key = np.stack([cos, sin], 1).reshape(HD, T).astype(np.float32)
    high = key.astype(bf)
    mid = (key - high.astype(np.float32)).astype(bf)
    low = (key - high.astype(np.float32) - mid.astype(np.float32)).astype(bf)
    k_rel = np.concatenate([(high, mid, low)[p] for p in K_PARTS] + [np.ones((2, T), bf)])

    ins = {"x": a(L0_attn_x), "weights": weights, "cols": cols, "rows": rows, "rel_tab": rel_tab, "k_rel": k_rel,
           "ident": np.eye(P, dtype=np.float32)}
    ins = {n: np.ascontiguousarray(v) for n, v in ins.items()}
    nc = bacc.Bacc("TRN2", target_bir_lowering=False, num_devices=1)
    aps = {n: nc.dram_tensor(n, v.shape, mybir.dt.from_np(v.dtype), kind="ExternalInput").ap() for n, v in ins.items()}
    out = nc.dram_tensor("out", (B, T, C), mybir.dt.float32, kind="ExternalOutput").ap()
    scratch = nc.dram_tensor("scratch", (2, 3, C, T), mybir.dt.bfloat16, kind="Internal").ap()
    build(nc, *(aps[n] for n in ("x", "weights", "cols", "rows", "rel_tab", "k_rel", "ident")), out, scratch)
    return run_bass_kernel_spmd(nc, [ins], core_ids=[0]).results[0]["out"]
```
